# Optimizing a Trainium2 kernel written in Bass

```python
import numpy as np
import jax
import jax.numpy as jnp

def _softmax(x, axis=-1):
    return jax.nn.softmax(x, axis=axis)

def _gelu(x):
    return jax.nn.gelu(x, approximate=True)

def _silu(x):
    return jax.nn.silu(x)

def _sigmoid(x):
    return jax.nn.sigmoid(x)

def _layernorm(x, axis=-1, eps=1e-05):
    m = jnp.mean(x, axis=axis, keepdims=True)
    v = jnp.var(x, axis=axis, keepdims=True)
    return (x - m) / jnp.sqrt(v + eps)

def _scatter_add(tgt, idx, src, axis=0):
    return tgt.at[idx].add(src)

def _segment_sum(src, seg, n):
    return jax.ops.segment_sum(src, seg, n)
kernel_name = 'mk_cond_seq_d2_seqx_r8_55c0b2'

def setup_inputs(seed: int=0):
    np.random.seed(seed)
    _w = jnp.asarray

    def _rec_inputs():
        import jax
        import jax.numpy as jnp
        _rk = jax.random.key(seed)
        x = -0.0002928 + 1 * jax.random.normal(jax.random.fold_in(_rk, 1), (32, 32, 128), jnp.float32)
        _lenS = 32 - jax.random.randint(jax.random.fold_in(_rk, 7), (32,), 0, max(1, 32 // 4) + 1, jnp.int32)
        _lenS2 = 32 - jax.random.randint(jax.random.fold_in(_rk, 8), (32,), 0, max(1, 32 // 4) + 1, jnp.int32)
        cond_1024 = 0.000887014 + 1.03683 * jax.random.normal(jax.random.fold_in(_rk, 11), (32, 128), jnp.float32)
        _validS = jnp.arange(32)[None, :] < _lenS[:, None]
        _validS2 = jnp.arange(32)[None, :] < _lenS2[:, None]
        _causal = jnp.tril(jnp.ones((32, 32), dtype=bool))
        mask_BxS_ik0 = jnp.where(jnp.broadcast_to(_validS[:, :], (32, 32)), 0, 1).astype(jnp.int32)
        return (x, cond_1024, mask_BxS_ik0)
    x, cond_1024, mask_BxS_ik0 = _rec_inputs()

    def _L0_cond_setup():
        import jax, jax.numpy as jnp
        import numpy as np
        EMBED = 128
        HEADS = 16
        HEAD_DIM = EMBED // HEADS
        MLP = 4 * EMBED
        EPS = 1e-06

        def _adaln(x, c, norm_w, scale_w, scale_b, shift_w, shift_b):
            sc = jax.nn.silu(c)
            shift = sc @ shift_w.T + shift_b
            scale = jnp.clip(sc @ scale_w.T + scale_b + 1.0, 0.1, 10.0)
            norm = jnp.maximum(jnp.linalg.norm(x, axis=-1, keepdims=True) * x.shape[-1] ** (-0.5), EPS)
            h = x / norm * norm_w
            return h * scale[:, None, :] + shift[:, None, :]

        def _attention(x, attention_mask, qkv_w, proj_w, proj_b):
            B, N, C = x.shape
            qkv = (x @ qkv_w.T).reshape(B, N, 3, HEADS, HEAD_DIM)
            q = qkv[:, :, 0].transpose(0, 2, 1, 3)
            k = qkv[:, :, 1].transpose(0, 2, 1, 3)
            v = qkv[:, :, 2].transpose(0, 2, 1, 3)
            attn = jnp.einsum('bhnd,bhmd->bhnm', q, k) * HEAD_DIM ** (-0.5)
            mask = attention_mask[:, None, None, :]
            attn = jnp.where(mask == 0, -jnp.inf, attn)
            all_inf = jnp.all(attn == -jnp.inf, axis=-1, keepdims=True)
            attn = jnp.where(all_inf, 0.0, attn)
            p = jax.nn.softmax(attn, axis=-1)
            out = jnp.einsum('bhnm,bhmd->bhnd', p, v).transpose(0, 2, 1, 3).reshape(B, N, C)
            return out @ proj_w.T + proj_b

        def _mlp(x, w1, b1, w2, b2):
            h = x @ w1.T + b1
            x1, x2 = jnp.split(h, 2, axis=-1)
            return jax.nn.silu(x1) * x2 @ w2.T + b2
        key = jax.random.key(seed)
        ks = jax.random.split(key, 16)
        B, N, C = (2, 256, EMBED)
        x = jax.random.normal(ks[0], (B, N, C), dtype=jnp.float32)
        c = jax.random.normal(ks[1], (B, C), dtype=jnp.float32)
        attention_mask = jax.random.randint(ks[2], (B, N), 0, 2, dtype=jnp.int32)
        s = 0.02
        params = {'norm_w': jnp.ones((C,), jnp.float32), 'scale_w': s * jax.random.normal(ks[3], (C, C), jnp.float32), 'scale_b': s * jax.random.normal(ks[4], (C,), jnp.float32), 'shift_w': s * jax.random.normal(ks[5], (C, C), jnp.float32), 'shift_b': s * jax.random.normal(ks[6], (C,), jnp.float32), 'qkv_w': s * jax.random.normal(ks[7], (3 * C, C), jnp.float32), 'proj_w': s * jax.random.normal(ks[8], (C, C), jnp.float32), 'proj_b': s * jax.random.normal(ks[9], (C,), jnp.float32), 'mlp_w1': s * jax.random.normal(ks[10], (2 * MLP, C), jnp.float32), 'mlp_b1': s * jax.random.normal(ks[11], (2 * MLP,), jnp.float32), 'mlp_w2': s * jax.random.normal(ks[12], (C, MLP), jnp.float32), 'mlp_b2': s * jax.random.normal(ks[13], (C,), jnp.float32)}
        return {'x': x, 'c': c, 'attention_mask': attention_mask, **params}
    _L0_cond_all = _L0_cond_setup()
    _L0_cond_in = {k: v for k, v in _L0_cond_all.items() if k in ('norm_w', 'scale_w', 'scale_b', 'shift_w', 'shift_b', 'qkv_w', 'proj_w', 'proj_b', 'mlp_w1', 'mlp_b1', 'mlp_w2', 'mlp_b2')}
    del _L0_cond_all

    def _L1_cond_setup():
        import jax, jax.numpy as jnp
        import numpy as np
        B, S, D, H, F = (4, 128, 128, 16, 512)
        EPS = 1e-06
        NEG = -1000000000.0

        def _mat(k, m, n):
            return jax.random.normal(k, (m, n), dtype=jnp.float32) / np.sqrt(m)

        def _ln(x, g, b):
            mu = jnp.mean(x, -1, keepdims=True)
            var = jnp.var(x, -1, keepdims=True)
            return (x - mu) * jax.lax.rsqrt(var + EPS) * g + b

        def _mha(x, wq, wk, wv, wo, bias):
            b, s, dm = x.shape
            dh = dm // H
            q = (x @ wq).reshape(b, s, H, dh)
            k = (x @ wk).reshape(b, s, H, dh)
            v = (x @ wv).reshape(b, s, H, dh)
            scores = jnp.einsum('bqhd,bkhd->bhqk', q, k) / np.sqrt(dh) + bias
            a = jax.nn.softmax(scores, axis=-1)
            o = jnp.einsum('bhqk,bkhd->bqhd', a, v).reshape(b, s, dm)
            return o @ wo

        def _biases(s):
            idx = jnp.arange(s)
            dist = jnp.abs(idx[:, None] - idx[None, :]).astype(jnp.float32)
            grid_bias = -dist
            reg_bias = jnp.where(dist <= 1, 0.0, NEG)
            ent_bias = jnp.where(idx[:, None] // 2 == idx[None, :] // 2, 0.0, NEG)
            sem_bias = jnp.zeros((s, s), jnp.float32)
            return (grid_bias, reg_bias, ent_bias, sem_bias)
        key = jax.random.key(seed)
        ks = jax.random.split(key, 32)
        d = {'x': jax.random.normal(ks[0], (B, S, D), dtype=jnp.float32), 't_emb': jax.random.normal(ks[1], (B, D), dtype=jnp.float32), 'ln1_g': jnp.ones((D,), jnp.float32), 'ln1_b': jnp.zeros((D,), jnp.float32), 'ln2_g': jnp.ones((D,), jnp.float32), 'ln2_b': jnp.zeros((D,), jnp.float32), 'ada_w': _mat(ks[2], D, 6 * D), 'ada_b': jnp.zeros((6 * D,), jnp.float32), 'fus_wg': _mat(ks[3], 4 * D, 4), 'fus_bg': jnp.zeros((4,), jnp.float32), 'fus_wo': _mat(ks[4], D, D), 'ffn_w1': _mat(ks[5], D, F), 'ffn_w2': _mat(ks[6], F, D), 'ffn_w3': _mat(ks[7], D, F)}
        i = 8
        for p in ('grid', 'reg', 'ent', 'sem'):
            for w in ('wq', 'wk', 'wv', 'wo'):
                d[f'{p}_{w}'] = _mat(ks[i], D, D)
                i += 1
        return d
    _L1_cond_all = _L1_cond_setup()
    _L1_cond_in = {k: v for k, v in _L1_cond_all.items() if k in ('ln1_g', 'ln1_b', 'ln2_g', 'ln2_b', 'ada_w', 'ada_b', 'grid_wq', 'grid_wk', 'grid_wv', 'grid_wo', 'reg_wq', 'reg_wk', 'reg_wv', 'reg_wo', 'ent_wq', 'ent_wk', 'ent_wv', 'ent_wo', 'sem_wq', 'sem_wk', 'sem_wv', 'sem_wo', 'fus_wg', 'fus_bg', 'fus_wo', 'ffn_w1', 'ffn_w2', 'ffn_w3')}
    del _L1_cond_all
    return {'x': x, 'cond_1024': cond_1024, 'mask_BxS_ik0': mask_BxS_ik0, 'L0_cond_norm_w': _L0_cond_in['norm_w'], 'L0_cond_scale_w': _L0_cond_in['scale_w'], 'L0_cond_scale_b': _L0_cond_in['scale_b'], 'L0_cond_shift_w': _L0_cond_in['shift_w'], 'L0_cond_shift_b': _L0_cond_in['shift_b'], 'L0_cond_qkv_w': _L0_cond_in['qkv_w'], 'L0_cond_proj_w': _L0_cond_in['proj_w'], 'L0_cond_proj_b': _L0_cond_in['proj_b'], 'L0_cond_mlp_w1': _L0_cond_in['mlp_w1'], 'L0_cond_mlp_b1': _L0_cond_in['mlp_b1'], 'L0_cond_mlp_w2': _L0_cond_in['mlp_w2'], 'L0_cond_mlp_b2': _L0_cond_in['mlp_b2'], 'L1_cond_ln1_g': _L1_cond_in['ln1_g'], 'L1_cond_ln1_b': _L1_cond_in['ln1_b'], 'L1_cond_ln2_g': _L1_cond_in['ln2_g'], 'L1_cond_ln2_b': _L1_cond_in['ln2_b'], 'L1_cond_ada_w': _L1_cond_in['ada_w'], 'L1_cond_ada_b': _L1_cond_in['ada_b'], 'L1_cond_grid_wq': _L1_cond_in['grid_wq'], 'L1_cond_grid_wk': _L1_cond_in['grid_wk'], 'L1_cond_grid_wv': _L1_cond_in['grid_wv'], 'L1_cond_grid_wo': _L1_cond_in['grid_wo'], 'L1_cond_reg_wq': _L1_cond_in['reg_wq'], 'L1_cond_reg_wk': _L1_cond_in['reg_wk'], 'L1_cond_reg_wv': _L1_cond_in['reg_wv'], 'L1_cond_reg_wo': _L1_cond_in['reg_wo'], 'L1_cond_ent_wq': _L1_cond_in['ent_wq'], 'L1_cond_ent_wk': _L1_cond_in['ent_wk'], 'L1_cond_ent_wv': _L1_cond_in['ent_wv'], 'L1_cond_ent_wo': _L1_cond_in['ent_wo'], 'L1_cond_sem_wq': _L1_cond_in['sem_wq'], 'L1_cond_sem_wk': _L1_cond_in['sem_wk'], 'L1_cond_sem_wv': _L1_cond_in['sem_wv'], 'L1_cond_sem_wo': _L1_cond_in['sem_wo'], 'L1_cond_fus_wg': _L1_cond_in['fus_wg'], 'L1_cond_fus_bg': _L1_cond_in['fus_bg'], 'L1_cond_fus_wo': _L1_cond_in['fus_wo'], 'L1_cond_ffn_w1': _L1_cond_in['ffn_w1'], 'L1_cond_ffn_w2': _L1_cond_in['ffn_w2'], 'L1_cond_ffn_w3': _L1_cond_in['ffn_w3']}

def reference(x, cond_1024, mask_BxS_ik0, L0_cond_norm_w, L0_cond_scale_w, L0_cond_scale_b, L0_cond_shift_w, L0_cond_shift_b, L0_cond_qkv_w, L0_cond_proj_w, L0_cond_proj_b, L0_cond_mlp_w1, L0_cond_mlp_b1, L0_cond_mlp_w2, L0_cond_mlp_b2, L1_cond_ln1_g, L1_cond_ln1_b, L1_cond_ln2_g, L1_cond_ln2_b, L1_cond_ada_w, L1_cond_ada_b, L1_cond_grid_wq, L1_cond_grid_wk, L1_cond_grid_wv, L1_cond_grid_wo, L1_cond_reg_wq, L1_cond_reg_wk, L1_cond_reg_wv, L1_cond_reg_wo, L1_cond_ent_wq, L1_cond_ent_wk, L1_cond_ent_wv, L1_cond_ent_wo, L1_cond_sem_wq, L1_cond_sem_wk, L1_cond_sem_wv, L1_cond_sem_wo, L1_cond_fus_wg, L1_cond_fus_bg, L1_cond_fus_wo, L1_cond_ffn_w1, L1_cond_ffn_w2, L1_cond_ffn_w3):
    import jax
    import jax.numpy as jnp

    def _L0_cond_ref(x, c, attention_mask, norm_w, scale_w, scale_b, shift_w, shift_b, qkv_w, proj_w, proj_b, mlp_w1, mlp_b1, mlp_w2, mlp_b2):
        import jax, jax.numpy as jnp
        import numpy as np
        EMBED = 128
        HEADS = 16
        HEAD_DIM = EMBED // HEADS
        MLP = 4 * EMBED
        EPS = 1e-06

        def _adaln(x, c, norm_w, scale_w, scale_b, shift_w, shift_b):
            sc = jax.nn.silu(c)
            shift = sc @ shift_w.T + shift_b
            scale = jnp.clip(sc @ scale_w.T + scale_b + 1.0, 0.1, 10.0)
            norm = jnp.maximum(jnp.linalg.norm(x, axis=-1, keepdims=True) * x.shape[-1] ** (-0.5), EPS)
            h = x / norm * norm_w
            return h * scale[:, None, :] + shift[:, None, :]

        def _attention(x, attention_mask, qkv_w, proj_w, proj_b):
            B, N, C = x.shape
            qkv = (x @ qkv_w.T).reshape(B, N, 3, HEADS, HEAD_DIM)
            q = qkv[:, :, 0].transpose(0, 2, 1, 3)
            k = qkv[:, :, 1].transpose(0, 2, 1, 3)
            v = qkv[:, :, 2].transpose(0, 2, 1, 3)
            attn = jnp.einsum('bhnd,bhmd->bhnm', q, k) * HEAD_DIM ** (-0.5)
            mask = attention_mask[:, None, None, :]
            attn = jnp.where(mask == 0, -jnp.inf, attn)
            all_inf = jnp.all(attn == -jnp.inf, axis=-1, keepdims=True)
            attn = jnp.where(all_inf, 0.0, attn)
            p = jax.nn.softmax(attn, axis=-1)
            out = jnp.einsum('bhnm,bhmd->bhnd', p, v).transpose(0, 2, 1, 3).reshape(B, N, C)
            return out @ proj_w.T + proj_b

        def _mlp(x, w1, b1, w2, b2):
            h = x @ w1.T + b1
            x1, x2 = jnp.split(h, 2, axis=-1)
            return jax.nn.silu(x1) * x2 @ w2.T + b2
        x = x + _attention(_adaln(x, c, norm_w, scale_w, scale_b, shift_w, shift_b), attention_mask, qkv_w, proj_w, proj_b)
        x = x + _mlp(_adaln(x, c, norm_w, scale_w, scale_b, shift_w, shift_b), mlp_w1, mlp_b1, mlp_w2, mlp_b2)
        return x

    def _L1_cond_ref(x, t_emb, ln1_g, ln1_b, ln2_g, ln2_b, ada_w, ada_b, grid_wq, grid_wk, grid_wv, grid_wo, reg_wq, reg_wk, reg_wv, reg_wo, ent_wq, ent_wk, ent_wv, ent_wo, sem_wq, sem_wk, sem_wv, sem_wo, fus_wg, fus_bg, fus_wo, ffn_w1, ffn_w2, ffn_w3):
        import jax, jax.numpy as jnp
        import numpy as np
        B, S, D, H, F = (4, 128, 128, 16, 512)
        EPS = 1e-06
        NEG = -1000000000.0

        def _mat(k, m, n):
            return jax.random.normal(k, (m, n), dtype=jnp.float32) / np.sqrt(m)

        def _ln(x, g, b):
            mu = jnp.mean(x, -1, keepdims=True)
            var = jnp.var(x, -1, keepdims=True)
            return (x - mu) * jax.lax.rsqrt(var + EPS) * g + b

        def _mha(x, wq, wk, wv, wo, bias):
            b, s, dm = x.shape
            dh = dm // H
            q = (x @ wq).reshape(b, s, H, dh)
            k = (x @ wk).reshape(b, s, H, dh)
            v = (x @ wv).reshape(b, s, H, dh)
            scores = jnp.einsum('bqhd,bkhd->bhqk', q, k) / np.sqrt(dh) + bias
            a = jax.nn.softmax(scores, axis=-1)
            o = jnp.einsum('bhqk,bkhd->bqhd', a, v).reshape(b, s, dm)
            return o @ wo

        def _biases(s):
            idx = jnp.arange(s)
            dist = jnp.abs(idx[:, None] - idx[None, :]).astype(jnp.float32)
            grid_bias = -dist
            reg_bias = jnp.where(dist <= 1, 0.0, NEG)
            ent_bias = jnp.where(idx[:, None] // 2 == idx[None, :] // 2, 0.0, NEG)
            sem_bias = jnp.zeros((s, s), jnp.float32)
            return (grid_bias, reg_bias, ent_bias, sem_bias)
        s = x.shape[1]
        gb, rb, eb, sb = _biases(s)
        ada = jax.nn.silu(t_emb) @ ada_w + ada_b
        sh_m, sc_m, g_m, sh_f, sc_f, g_f = jnp.split(ada, 6, axis=1)
        nx = _ln(x, ln1_g, ln1_b) * (1 + sc_m[:, None, :]) + sh_m[:, None, :]
        o1 = _mha(nx, grid_wq, grid_wk, grid_wv, grid_wo, gb)
        o2 = _mha(nx, reg_wq, reg_wk, reg_wv, reg_wo, rb)
        o3 = _mha(nx, ent_wq, ent_wk, ent_wv, ent_wo, eb)
        o4 = _mha(nx, sem_wq, sem_wk, sem_wv, sem_wo, sb)
        gate = jax.nn.softmax(jnp.concatenate([o1, o2, o3, o4], axis=-1) @ fus_wg + fus_bg, axis=-1)
        fused = (gate[..., 0:1] * o1 + gate[..., 1:2] * o2 + gate[..., 2:3] * o3 + gate[..., 3:4] * o4) @ fus_wo
        x = x + g_m[:, None, :] * fused
        nx2 = _ln(x, ln2_g, ln2_b) * (1 + sc_f[:, None, :]) + sh_f[:, None, :]
        ffn = jax.nn.silu(nx2 @ ffn_w1) * (nx2 @ ffn_w3) @ ffn_w2
        return x + g_f[:, None, :] * ffn
    x = _L0_cond_ref(x, cond_1024, mask_BxS_ik0, L0_cond_norm_w, L0_cond_scale_w, L0_cond_scale_b, L0_cond_shift_w, L0_cond_shift_b, L0_cond_qkv_w, L0_cond_proj_w, L0_cond_proj_b, L0_cond_mlp_w1, L0_cond_mlp_b1, L0_cond_mlp_w2, L0_cond_mlp_b2)
    x = _L1_cond_ref(x, cond_1024, L1_cond_ln1_g, L1_cond_ln1_b, L1_cond_ln2_g, L1_cond_ln2_b, L1_cond_ada_w, L1_cond_ada_b, L1_cond_grid_wq, L1_cond_grid_wk, L1_cond_grid_wv, L1_cond_grid_wo, L1_cond_reg_wq, L1_cond_reg_wk, L1_cond_reg_wv, L1_cond_reg_wo, L1_cond_ent_wq, L1_cond_ent_wk, L1_cond_ent_wv, L1_cond_ent_wo, L1_cond_sem_wq, L1_cond_sem_wk, L1_cond_sem_wv, L1_cond_sem_wo, L1_cond_fus_wg, L1_cond_fus_bg, L1_cond_fus_wo, L1_cond_ffn_w1, L1_cond_ffn_w2, L1_cond_ffn_w3)
    return x

_drawn_inputs = setup_inputs


def setup_inputs(seed=0):
    import zlib

    import numpy as np

    out = dict(_drawn_inputs(seed))
    spreads = {'L0_cond_norm_w': (1.0, 0.6),
     'L1_cond_ln1_g': (1.0, 0.2),
     'L1_cond_ln1_b': (0.0, 0.412),
     'L1_cond_ln2_g': (1.0, 0.2),
     'L1_cond_ln2_b': (0.0, 0.301),
     'L1_cond_ada_b': (0.0, 0.1),
     'L1_cond_fus_bg': (0.0, 1.87)}
    factors = {'L0_cond_scale_w': 8.0,
     'L0_cond_scale_b': 8.0,
     'L0_cond_shift_w': 5.91,
     'L0_cond_shift_b': 8.0,
     'L0_cond_mlp_w1': 3.555,
     'L0_cond_mlp_b1': 8.0,
     'L0_cond_mlp_w2': 3.551,
     'L0_cond_mlp_b2': 8.0}
    for name, (base, spread) in spreads.items():
        noise = np.random.default_rng([zlib.crc32(name.encode()), seed]).standard_normal(out[name].shape)
        drawn = base * np.exp(spread * noise) if base else spread * noise
        out[name] = jnp.asarray(drawn.astype(out[name].dtype))
    for name, factor in factors.items():
        out[name] = (out[name] * factor).astype(out[name].dtype)
    return out
```

```python
from contextlib import ExitStack

import concourse.bass as bass
from concourse import mybir

F32 = mybir.dt.float32
BF16 = mybir.dt.bfloat16
ALU = mybir.AluOpType
ACT = mybir.ActivationFunctionType
AX_X = mybir.AxisListType.X

P = 128
S = 32
C = 128
HEADS = 16
HD = C // HEADS
SEQS = P // S
J = 4
G = HEADS // J
SLOTS = 8
M = 4
F = 512
FC = F // P
VW = HD + 1
SCALE = float(HD) ** -0.5
RMS_EPS = 1e-6
LN_EPS = 1e-6
MASKED = 2.0 ** 126

EARLY = {"ident": P, "same_q": P, "same_b": P, "key_of": S, "bias": 3 * S, "slot_mask": SLOTS, "j_mask": J,
         "shift_w": C, "scale_w": C, "norm_w": 1, "scale_b": 1, "shift_b": 1}
L0 = {"qkv": 3 * C, "proj": C}
MLP = {"w1": 2 * F, "w2": F, "b1": 2 * FC}
ADA = {"ada_w": 6 * C, "ada_b": 6, "ln1_g": 1, "ln1_b": 1, "ln2_g": 1, "ln2_b": 1, "fus_wo": C,
       "fus_wg": M * M, "wo_t": M * C}
QKV1 = {"wq": M * C, "wk": M * C, "wv": M * C}
FFN = {"w1": F, "w3": F, "w2": F}
ROWS = {"proj_b": C, "mlp_b2": C, "gate_b": 2 * C, "fus_bg": M}


def columns(layout):
    at, out = 0, {}
    for name, n in layout.items():
        out[name] = slice(at, at + n)
        at += n
    return out, at


def build(nc, x, cond, mask, early, l0, mlp, ada, qkv1, ffn, rows, out):
    TILES = x.shape[0] // P
    B = cond.shape[0]

    with ExitStack() as ctx:
        def sb(name, shape, dt=F32):
            return ctx.enter_context(nc.sbuf_tensor(name, shape, dt))

        def sem(name):
            return ctx.enter_context(nc.semaphore(name))

        packs = {}
        for name, layout in (("early", EARLY), ("l0", L0), ("mlp", MLP), ("ada", ADA), ("qkv1", QKV1), ("ffn", FFN), ("rows", ROWS)):
            cols, n = columns(layout)
            packs[name] = (sb(f"w_{name}", [P, n]), cols)

        def w(pack, name):
            t, cols = packs[pack]
            return t[:, cols[name]]

        ident = w("early", "ident")
        slot_mask, j_mask = w("early", "slot_mask"), w("early", "j_mask")
        same_q16 = sb("same_q16", [P, P], BF16)
        same_b16 = sb("same_b16", [P, P], BF16)
        bias16 = sb("bias16", [P, 3, S], BF16)
        mask16 = sb("mask16", [P, TILES, S], BF16)
        ones = sb("ones", [P, P])
        neg_half = sb("neg_half", [P, 1])
        mask_raw = sb("mask_raw", [P, TILES], mybir.dt.int32)
        attended = sb("attended", [P, TILES])
        attended_b = sb("attended_b", [P, TILES, SEQS])
        any_key = sb("any_key", [P, TILES])
        mask_add = sb("mask_add", [P, TILES])
        q_scale = sb("q_scale", [P, B])
        cond_sb = sb("cond_sb", [B, C])
        cond_tanh = sb("cond_tanh", [B, C])
        cond_silu = sb("cond_silu", [B, C])
        cond_t = sb("cond_t", [P, B])
        cond_tok = sb("cond_tok", [P, B, S])
        mod = sb("mod", [P, 6, B])
        scale1 = sb("scale1", [P, B])
        gates = sb("gates", [P, TILES, 2 * C])
        wo_fused = sb("wo_fused", [P, M, C + M])

        z_x = sb("z_x", [P, C])
        z_xb = sb("z_xb", [P, C])
        z_sq = sb("z_sq", [P, C])
        z_ss = sb("z_ss", [P, 1])
        z_ms = sb("z_ms", [P, 1])
        z_rn = sb("z_rn", [P, 1])
        z_xn = sb("z_xn", [P, C])
        z_xs = sb("z_xs", [P, P])
        z_h = sb("z_h", [P, P])
        z_q = sb("z_q", [P, 2, P])
        z_k = sb("z_k", [P, P])
        z_ks = sb("z_ks", [P, SLOTS, P])
        z_v = sb("z_v", [P, SEQS, G, HD])
        z_vs = sb("z_vs", [P, SEQS, G, J, VW])
        z_x1 = sb("z_x1", [P, C])
        z_x1b = sb("z_x1b", [P, C])
        z_h1 = sb("z_h1", [P, FC, P])
        z_h2 = sb("z_h2", [P, FC, P])
        z_th = sb("z_th", [P, FC, P])
        z_g = sb("z_g", [P, FC, P])
        z_y = sb("z_y", [P, C])
        a_x = sb("a_x", [P, C])
        a_st = sb("a_st", [P, 6])
        a_mv = sb("a_mv", [P, 2])
        a_ve = sb("a_ve", [P, 1])
        a_rs = sb("a_rs", [P, 1])
        a_xn = sb("a_xn", [P, C])
        a_xs = sb("a_xs", [P, P])
        a_h = sb("a_h", [P, P])
        a_q = sb("a_q", [P, M, 2, P])
        a_k = sb("a_k", [P, M, P])
        a_ks = sb("a_ks", [P, M, SLOTS, P])
        a_v = sb("a_v", [P, M, SEQS, G, HD])
        a_vs = sb("a_vs", [P, M, SEQS, G, J, VW])
        a_y = sb("a_y", [P, M, C + M])
        a_lg = sb("a_lg", [P, M])
        a_lb = sb("a_lb", [P, M])
        a_lm = sb("a_lm", [P, 1])
        a_le = sb("a_le", [P, M])
        a_ls = sb("a_ls", [P, 1])
        a_lr = sb("a_lr", [P, 1])
        a_f = sb("a_f", [P, M, C])
        a_fg = sb("a_fg", [P, C])
        f_x = sb("f_x", [P, C])
        f_st = sb("f_st", [P, 6])
        f_mv = sb("f_mv", [P, 2])
        f_ve = sb("f_ve", [P, 1])
        f_rs = sb("f_rs", [P, 1])
        f_xn = sb("f_xn", [P, C])
        f_xs = sb("f_xs", [P, P])
        f_h = sb("f_h", [P, P])
        f_th = sb("f_th", [P, F])
        f_v = sb("f_v", [P, F])
        f_g = sb("f_g", [P, FC, P])
        f_y = sb("f_y", [P, C])
        f_out = sb("f_out", [P, C])
        u_max = [sb(f"u_max{n}", [P, HEADS]) for n in range(2)]
        u_p = [sb(f"u_p{n}", [P, HEADS, S]) for n in range(2)]
        u_pt = [sb(f"u_pt{n}", [P, G, P]) for n in range(2)]
        u_r = [sb(f"u_r{n}", [P, HEADS]) for n in range(2)]
        u_o = [sb(f"u_o{n}", [P, C]) for n in range(2)]
        u_ot = [sb(f"u_ot{n}", [P, P]) for n in range(2)]

        def ps(name):
            return ctx.enter_context(nc.psum_tensor(name, [P, 512], F32))

        ps_s = [ps("ps_s0"), ps("ps_s1")]
        ps_t = [ps("ps_t0"), ps("ps_t1")]
        ps_o = [ps("ps_o0"), ps("ps_o1")]
        g0, g1 = ps("ps_g0"), ps("ps_g1")

        in_x = sem("in_x")
        in_ = {n: sem(f"in_{n}") for n in ("cond", "mask", *packs)}
        out_stored = sem("out_stored")
        set_dve, set_pe, set_act, set_pool = sem("set_dve"), sem("set_pe"), sem("set_act"), sem("set_pool")

        z_ss_ok, z_ms_ok, z_rn_ok, z_xn_ok = sem("z_ss_ok"), sem("z_ms_ok"), sem("z_rn_ok"), sem("z_xn_ok")
        z_turned, z_scaled, z_h_ok = sem("z_turned"), sem("z_scaled"), sem("z_h_ok")
        z_xb_ok, z_qkv, z_qkv_read, z_ks_ok, z_vs_ok = (sem(n) for n in ("z_xb_ok", "z_qkv", "z_qkv_read", "z_ks_ok", "z_vs_ok"))
        z_x1_ok, z_x1b_ok = sem("z_x1_ok"), sem("z_x1b_ok")
        z_up = sem("z_up")
        z_h1_ok, z_h2_ok, z_th_ok, z_act_ok, z_g_ok = (sem(n) for n in ("z_h1_ok", "z_h2_ok", "z_th_ok", "z_act_ok", "z_g_ok"))
        z_down, z_y_ok = sem("z_down"), sem("z_y_ok")
        a_x_ok, a_mv_ok, a_ve_ok, a_rs_ok, a_xn_ok, a_turned, a_scaled, a_h_ok = (
            sem(f"a_{n}") for n in ("x_ok", "mv_ok", "ve_ok", "rs_ok", "xn_ok", "turned", "scaled", "h_ok"))
        a_q_ps, a_q_ok, a_k_ps, a_k_ok, a_v_ps, a_v_ok = (sem(f"a_{n}") for n in ("q_ps", "q_ok", "k_ps", "k_ok", "v_ps", "v_ok"))
        a_ks_ok, a_vs_ok = sem("a_ks_ok"), sem("a_vs_ok")
        a_lg_ok, a_lb_ok, a_lm_ok, a_le_ok, a_lr_ok, a_fg_ok = (sem(f"a_{n}") for n in ("lg_ok", "lb_ok", "lm_ok", "le_ok", "lr_ok", "fg_ok"))
        a_f_ok = sem("a_f_ok")
        a_x1_ok = sem("a_x1_ok")
        f_mv_ok, f_ve_ok, f_rs_ok, f_xn_ok, f_turned, f_scaled, f_h_ok = (
            sem(f"f_{n}") for n in ("mv_ok", "ve_ok", "rs_ok", "xn_ok", "turned", "scaled", "h_ok"))
        f_up = sem("f_up")
        f_th_ok, f_v_ok, f_g_ok, f_down, f_y_ok, f_out_ok = (sem(f"f_{n}") for n in ("th_ok", "v_ok", "g_ok", "down", "y_ok", "out_ok"))
        u_scored, u_max_ok, u_sub, u_exp, u_turned, u_pt_ok, u_pv, u_r_ok, u_o_ok, u_oturned, u_ot_ok, u_y, u_y_read = (
            [sem(f"u_{n}{lane}") for lane in range(2)] for n in
            ("scored", "max", "sub", "exp", "turned", "pt_ok", "pv", "r_ok", "o_ok", "oturned", "ot_ok", "y", "y_read"))

        def at_least(eng, semaphore, count):
            if not isinstance(count, int) or count > 0:
                eng.wait_ge(semaphore, count)

        def use_a(i, m, z=True):
            if m in (0, 3):
                return 0, 3 * i + (1 if m == 0 else 3 if z else 2)
            return 1, 2 * i + m - 1

        def use_z(t):
            return 0, (t - 1) * 3 + 2 if not isinstance(t, int) or t > 0 else 0

        block = ctx.enter_context(nc.Block())

        @block.sync
        def _(sp):
            def load_x(t):
                sp.dma_start(z_x[:, :], x[bass.ts(t, P), :]).then_inc(in_x, 16)

            def load(name, src):
                sp.dma_start(packs[name][0][:, :], src).then_inc(in_[name], 16)

            load_x(0)
            load("early", early)
            sp.dma_start(cond_sb[:, :], cond).then_inc(in_["cond"], 16)
            sp.dma_start(mask_raw[:, :], mask).then_inc(in_["mask"], 16)
            load("l0", l0)
            sp.dma_start(packs["rows"][0][:, :], rows.to_broadcast([P, rows.shape[1]])).then_inc(in_["rows"], 16)
            load("mlp", mlp)
            load("ada", ada)
            load("qkv1", qkv1)
            load("ffn", ffn)

            def next_x(t):
                sp.wait_ge(z_xn_ok, 2 * t - 1)
                sp.wait_ge(z_xb_ok, t)
                load_x(t)

            def store(t):
                sp.wait_ge(f_out_ok, t + 1)
                sp.dma_start(out[bass.ts(t, P), :], f_out[:, :]).then_inc(out_stored, 16)

            next_x(1)
            for i in range(2):
                if i > 0:
                    store(i - 1)
                next_x(i + 2)
            with sp.Fori(2, TILES - 2) as i:
                store(i - 1)
                next_x(i + 2)
            for i in range(TILES - 2, TILES + 1):
                store(i - 1)
            sp.wait_ge(out_stored, 16 * TILES)

        @block.tensor
        def _(pe):
            mm = pe.matmul

            pe.wait_ge(set_dve, 4)
            pe.wait_ge(in_["early"], 16)
            mm(g1[:, 0:TILES], w("early", "same_b"), attended[:, :], start=True, stop=True)
            mm(g1[:, 32:32 + B], ones[:, :], attended_b[:, :, :], start=True, stop=True).then_inc(set_pe, 1)
            pe.wait_ge(set_dve, 5)
            pe.transpose(g0[:, 0:B], cond_silu[:, :], ident[0:B, 0:B]).then_inc(set_pe, 1)
            pe.wait_ge(set_act, 2)
            mm(g0[:, 32:32 + B], w("early", "shift_w"), cond_t[:, :], start=True, stop=True)
            mm(g0[:, 64:64 + B], w("early", "scale_w"), cond_t[:, :], start=True, stop=True).then_inc(set_pe, 1)

            def rest_of_setup():
                pe.wait_ge(in_["ada"], 16)
                pe.wait_ge(z_y_ok, 1)
                for n, part in enumerate((0, 1, 3, 4)):
                    last = mm(g0[:, n * B:n * B + B], w("ada", "ada_w")[:, part * C:part * C + C], cond_t[:, :],
                              start=True, stop=True)
                last.then_inc(set_pe, 1)
                for m in range(M):
                    if m > 0:
                        pe.wait_ge(set_act, 3 + m)
                    wo_t = w("ada", "wo_t")[:, m * C:m * C + C]
                    mm(g1[:, 0:C], wo_t, w("ada", "fus_wo"), start=True, stop=True)
                    mm(g1[:, C:C + M], wo_t, w("ada", "fus_wg")[:, m * M:m * M + M], start=True, stop=True).then_inc(set_pe, 1)
                for t in range(TILES):
                    bank = (g0, g1)[t % 2]
                    pe.wait_ge(set_dve, 10 + max(t - 1, 0))
                    if t == 1:
                        pe.wait_ge(set_act, 3 + M)
                    per_token = cond_tok[:, SEQS * t:SEQS * t + SEQS, :]
                    g_m, g_f = w("ada", "ada_w")[:, 2 * C:3 * C], w("ada", "ada_w")[:, 5 * C:6 * C]
                    mm(bank[:, 0:C], per_token, g_m, start=True, stop=True)
                    mm(bank[:, C:2 * C], per_token, g_f, start=True, stop=True).then_inc(set_pe, 1)
                pe.wait_ge(set_dve, 10 + TILES)

            def scores(lane, n, q, ks, bias_w=None, bias=None):
                at_least(pe, u_sub[lane], n)
                bank = ps_s[lane]
                if bias is not None:
                    mm(bank[:, :], bias_w[:, :], bias.unsqueeze(1).to_broadcast([P, HEADS, S]),
                       start=True, stop=False, skip_group_check=True)
                half = SLOTS * S
                for s in range(2):
                    for b in range(SEQS):
                        tok = slice(b * S, b * S + S)
                        last = mm(bank[tok, s * half:s * half + half], q[:, s, tok], ks[:, :, tok],
                                  start=bias is None, stop=True, skip_group_check=True)
                last.then_inc(u_scored[lane], 1)

            def turn(lane, n):
                pe.wait_ge(u_exp[lane], n + 1)
                at_least(pe, u_pt_ok[lane], n)
                for g in range(G):
                    last = pe.transpose(ps_t[lane][:, g * P:g * P + P], u_p[lane][:, g * J:g * J + J, :], ident)
                last.then_inc(u_turned[lane], 1)

            def weigh(lane, n, vs):
                pe.wait_ge(u_pt_ok[lane], n + 1)
                at_least(pe, u_y_read[lane], n)
                for g in range(G):
                    for b in range(SEQS):
                        tok = slice(b * S, b * S + S)
                        last = mm(ps_o[lane][tok, g * J * VW:(g + 1) * J * VW], u_pt[lane][:, g, tok],
                                  vs[:, b, g, :, :], start=True, stop=True, skip_group_check=True)
                last.then_inc(u_pv[lane], 1)

            def turn_out(lane, n):
                pe.wait_ge(u_o_ok[lane], n + 1)
                pe.transpose(ps_o[lane][:, 0:P], u_o[lane][:, :], ident).then_inc(u_oturned[lane], 1)

            def project(lane, n, weights):
                pe.wait_ge(u_ot_ok[lane], n + 1)
                mm(ps_o[lane][:, 0:weights.shape[1]], u_ot[lane][:, :], weights, start=True, stop=True).then_inc(u_y[lane], 1)

            def a_scores(i, m, z):
                lane, n = use_a(i, m, z)
                if m == 0:
                    pe.wait_ge(a_q_ok, i + 1)
                pe.wait_ge(a_ks_ok, M * i + m + 1)
                if m < 3:
                    scores(lane, n, a_q[:, m, :, :], a_ks[:, m, :, :], same_q16, bias16[:, m, :])
                else:
                    scores(lane, n, a_q[:, m, :, :], a_ks[:, m, :, :])

            def a_turn(i, m, z):
                turn(*use_a(i, m, z))

            def a_weigh(i, m, z):
                pe.wait_ge(a_vs_ok, M * i + m + 1)
                weigh(*use_a(i, m, z), a_vs[:, m, :, :, :, :])

            def a_turn_out(i, m, z):
                turn_out(*use_a(i, m, z))

            def a_project(i, m, z):
                project(*use_a(i, m, z), wo_fused[:, m, :])

            def z_turn_x(t, k):
                pe.wait_ge(z_xn_ok, 2 * t + k + 1)
                pe.transpose((g0, g1)[k][:, 0:P], z_xn[:, :], ident).then_inc(z_turned, 1)

            def z_project_qkv(t):
                pe.wait_ge(z_h_ok, 2 * t + 1)
                qkv = w("l0", "qkv")
                mm(g1[:, 0:P], qkv[:, 0:C], z_h[:, :], start=True, stop=True)
                mm(g1[:, P:2 * P], qkv[:, C:2 * C], z_h[:, :], start=True, stop=True)
                wv = qkv[:, 2 * C:].rearrange("c (g j d) -> c g j d", g=G, j=J)
                vw = G * HD
                for b in range(SEQS):
                    for j in range(J):
                        last = mm(g1[j * S:j * S + S, 2 * P + b * vw:2 * P + (b + 1) * vw],
                                  z_h[:, b * S:b * S + S], wv[:, :, j, :], start=True, stop=True, skip_group_check=True)
                last.then_inc(z_qkv, 1)

            def z_scores(t):
                pe.wait_ge(z_qkv_read, t + 1)
                pe.wait_ge(z_ks_ok, t + 1)
                lane, n = use_z(t)
                scores(lane, n, z_q, z_ks, same_b16, mask16[:, bass.ds(t, 1), :].rearrange("p o k -> p (o k)"))

            def z_turn(t):
                turn(*use_z(t))

            def z_weigh(t):
                pe.wait_ge(z_vs_ok, t + 1)
                weigh(*use_z(t), z_vs)

            def z_turn_out(t):
                turn_out(*use_z(t))

            def z_project(t):
                project(*use_z(t), w("l0", "proj"))

            def z_mlp_up(t):
                pe.wait_ge(z_h_ok, 2 * t + 2)
                for half, bank in enumerate((g0, g1)):
                    for c in range(FC):
                        col = (half * FC + c) * P
                        last = mm(bank[:, c * P:c * P + P], w("mlp", "w1")[:, col:col + P], z_h[:, :], start=True, stop=True)
                    last.then_inc(z_up, 1)

            def z_mlp_down(t):
                pe.wait_ge(z_g_ok, t + 1)
                for c in range(FC):
                    last = mm(g0[:, 0:C], z_g[:, c, :], w("mlp", "w2")[:, c * C:c * C + C], start=c == 0, stop=c == FC - 1)
                last.then_inc(z_down, 1)

            def a_turn_x(t):
                pe.wait_ge(a_xn_ok, t + 1)
                pe.transpose(g1[:, 0:P], a_xn[:, :], ident).then_inc(a_turned, 1)

            def a_project_qk(t):
                pe.wait_ge(a_h_ok, t + 1)
                for bank, name, full in ((g0, "wq", a_q_ps), (g1, "wk", a_k_ps)):
                    for m in range(M):
                        last = mm(bank[:, m * P:m * P + P], w("qkv1", name)[:, m * C:m * C + C], a_h[:, :], start=True, stop=True)
                    last.then_inc(full, 1)

            def a_project_v(t):
                pe.wait_ge(a_q_ok, t + 1)
                wv = w("qkv1", "wv").rearrange("c (m g j d) -> c m g j d", m=M, g=G, j=J)
                bank = g0[:, :].rearrange("p (m b v) -> p m b v", m=M, b=SEQS)
                for b in range(SEQS):
                    for j in range(J):
                        last = mm(bank[j * S:j * S + S, :, b, :], a_h[:, b * S:b * S + S],
                                  wv[:, :, :, j, :].rearrange("c m g d -> c (m g) d"), start=True, stop=True, skip_group_check=True)
                last.then_inc(a_v_ps, 1)

            def f_turn_x(t):
                pe.wait_ge(f_xn_ok, t + 1)
                pe.transpose(g1[:, 0:P], f_xn[:, :], ident).then_inc(f_turned, 1)

            def f_ffn_up(t):
                pe.wait_ge(f_h_ok, t + 1)
                for bank, name in ((g1, "w1"), (g0, "w3")):
                    for c in range(FC):
                        last = mm(bank[:, c * P:c * P + P], w("ffn", name)[:, c * P:c * P + P], f_h[:, :], start=True, stop=True)
                    last.then_inc(f_up, 1)

            def f_ffn_down(t):
                pe.wait_ge(f_g_ok, t + 1)
                for c in range(FC):
                    last = mm(g0[:, 0:C], f_g[:, c, :], w("ffn", "w2")[:, c * C:c * C + C], start=c == 0, stop=c == FC - 1)
                last.then_inc(f_down, 1)

            def iteration(i, z=True, f=True):
                a_project_qk(i)
                a_project_v(i)
                if f:
                    pe.wait_ge(a_k_ok, i + 1)
                    f_turn_x(i - 1)
                if z:
                    pe.wait_ge(a_v_ok, i + 1)
                    z_turn_x(i + 1, 0)
                if f:
                    if z:
                        pe.wait_ge(z_scaled, 2 * i + 3)
                    else:
                        pe.wait_ge(a_v_ok, i + 1)
                    f_ffn_up(i - 1)
                if z:
                    if f:
                        pe.wait_ge(f_v_ok, i)
                    else:
                        pe.wait_ge(a_k_ok, i + 1)
                    z_project_qkv(i + 1)
                a_scores(i, 0, z)
                a_scores(i, 1, z)
                if f:
                    f_ffn_down(i - 1)
                a_turn(i, 0, z)
                if z:
                    z_scores(i + 1)
                a_weigh(i, 0, z)
                a_turn(i, 1, z)
                a_scores(i, 2, z)
                a_turn_out(i, 0, z)
                a_weigh(i, 1, z)
                if z:
                    z_turn(i + 1)
                a_project(i, 0, z)
                a_scores(i, 3, z)
                if z:
                    z_weigh(i + 1)
                a_turn(i, 2, z)
                a_turn_out(i, 1, z)
                if z:
                    z_turn_out(i + 1)
                a_project(i, 1, z)
                if z:
                    z_project(i + 1)
                a_weigh(i, 2, z)
                a_turn(i, 3, z)
                if z:
                    z_turn_x(i + 1, 1)
                a_turn_out(i, 2, z)
                a_weigh(i, 3, z)
                a_project(i, 2, z)
                if z:
                    if f:
                        pe.wait_ge(f_y_ok, i)
                    else:
                        pe.wait_ge(z_scaled, 2 * i + 3)
                    z_mlp_up(i + 1)
                a_turn_out(i, 3, z)
                a_project(i, 3, z)
                if z:
                    z_mlp_down(i + 1)
                    a_turn_x(i + 1)

            z_turn_x(0, 0)
            pe.wait_ge(in_["l0"], 16)
            z_project_qkv(0)
            z_scores(0)
            z_turn(0)
            z_weigh(0)
            z_turn_out(0)
            z_project(0)
            z_turn_x(0, 1)
            pe.wait_ge(in_["mlp"], 16)
            z_mlp_up(0)
            z_mlp_down(0)
            rest_of_setup()
            pe.wait_ge(in_["qkv1"], 16)
            pe.wait_ge(in_["ffn"], 16)
            a_turn_x(0)
            iteration(0, f=False)
            iteration(1)
            with pe.Fori(2, TILES - 1) as i:
                iteration(i)
            iteration(TILES - 1, z=False)
            f_turn_x(TILES - 1)
            pe.wait_ge(f_y_ok, TILES - 1)
            f_ffn_up(TILES - 1)
            f_ffn_down(TILES - 1)

        @block.vector
        def _(dve):
            tt, ts, stt = dve.tensor_tensor, dve.tensor_scalar, dve.scalar_tensor_tensor
            neg_bias = packs["rows"]

            dve.memset(ones[:, :], 1.0).then_inc(set_dve, 1)
            dve.memset(neg_half[:, :], -0.5).then_inc(set_dve, 1)
            dve.wait_ge(in_["mask"], 16)
            ts(attended[:, :], mask_raw[:, :], 0.0, None, ALU.not_equal).then_inc(set_dve, 1)
            dve.wait_ge(set_dve, 3)
            dve.wait_ge(in_["early"], 16)
            tt(attended_b[:, :, :], attended[:, :].unsqueeze(2).to_broadcast([P, TILES, SEQS]),
               j_mask.unsqueeze(1).to_broadcast([P, TILES, SEQS]), ALU.mult).then_inc(set_dve, 1)
            dve.wait_ge(set_act, 1)
            stt(cond_silu[:, :], cond_tanh[:, :], 1.0, cond_sb[:, :], ALU.add, ALU.mult).then_inc(set_dve, 1)
            dve.wait_ge(set_pe, 1)
            ts(any_key[:, :], g1[:, 0:TILES], 1.0, MASKED, ALU.min, ALU.mult).then_inc(set_dve, 1)
            ts(q_scale[:, :], g1[:, 32:32 + B], 1.0, SCALE, ALU.min, ALU.mult).then_inc(set_dve, 1)
            dve.wait_ge(set_dve, 7)
            stt(mask_add[:, :], attended[:, :], 1.0, any_key[:, :], ALU.subtract, ALU.mult).then_inc(set_dve, 1)
            dve.wait_ge(set_dve, 8)
            set_chain = sem("set_chain")
            chain = [0]

            def then(ins):
                chain[0] += 1
                ins.then_inc(set_chain, 1)
                dve.wait_ge(set_chain, chain[0])

            then(tt(mask16[:, :, :], w("early", "key_of").unsqueeze(1).to_broadcast([P, TILES, S]),
                    mask_add[:, :].unsqueeze(2).to_broadcast([P, TILES, S]), ALU.mult))
            then(dve.tensor_copy(same_b16[:, :], w("early", "same_b")))
            dve.tensor_copy(same_q16[:, :], w("early", "same_q")).then_inc(set_chain, 1)
            dve.tensor_copy(bias16[:, :, :].rearrange("p m k -> p (m k)"), w("early", "bias")).then_inc(set_chain, 1)
            chain[0] += 2
            dve.wait_ge(set_pe, 3)
            ts(mod[:, 1, :], g0[:, 32:32 + B], w("early", "shift_b"), None, ALU.add).then_inc(set_chain, 1)
            chain[0] += 1
            then(ts(scale1[:, :], g0[:, 64:64 + B], w("early", "scale_b"), 1.0, ALU.add, ALU.add))
            then(ts(scale1[:, :], scale1[:, :], 0.1, 10.0, ALU.max, ALU.min))
            then(ts(mod[:, 0, :], scale1[:, :], w("early", "norm_w"), None, ALU.mult))
            for m in range(M):
                dve.tensor_copy(a_vs[:, m, :, :, :, HD].rearrange("p b g j -> p (b g) j"),
                                j_mask.unsqueeze(1).to_broadcast([P, SEQS * G, J])).then_inc(set_chain, 1)
            chain[0] += M
            dve.wait_ge(set_pool, 2)
            dve.tensor_copy(z_vs[:, :, :, :, HD].rearrange("p b g j -> p (b g) j"),
                            j_mask.unsqueeze(1).to_broadcast([P, SEQS * G, J])).then_inc(set_dve, 1)
            dve.wait_ge(set_dve, 9)

            def rest_of_setup():
                dve.wait_ge(in_["ada"], 16)
                dve.wait_ge(set_pe, 4)
                for n, (g, b) in enumerate((("ln1_g", "ln1_b"), ("ln2_g", "ln2_b"))):
                    sh, sc = 2 * n, 2 * n + 1
                    part = (0, 1, 3, 4)
                    ada_b = w("ada", "ada_b")
                    then(ts(scale1[:, :], g0[:, sc * B:sc * B + B], ada_b[:, part[sc]:part[sc] + 1], 1.0, ALU.add, ALU.add))
                    then(ts(mod[:, 2 + 2 * n, :], scale1[:, :], w("ada", g), None, ALU.mult))
                    then(ts(mod[:, 3 + 2 * n, :], g0[:, sh * B:sh * B + B], ada_b[:, part[sh]:part[sh] + 1], None, ALU.add))
                    last = stt(mod[:, 3 + 2 * n, :], scale1[:, :], w("ada", b), mod[:, 3 + 2 * n, :], ALU.mult, ALU.add)
                    if n == 0:
                        then(last)
                last.then_inc(set_dve, 1)
                dve.wait_ge(in_["rows"], 16)
                for t in range(TILES):
                    dve.wait_ge(set_pe, 5 + M + t)
                    tt(gates[:, t, :], (g0, g1)[t % 2][:, 0:2 * C], gate_b, ALU.add).then_inc(set_dve, 1)

            rows_sb, row_cols = packs["rows"]
            gate_b, fus_bg = rows_sb[:, row_cols["gate_b"]], rows_sb[:, row_cols["fus_bg"]]

            def softmax(lane, n):
                dve.wait_ge(u_scored[lane], n + 1)
                s = ps_s[lane][:, :].rearrange("p (h k) -> p h k", h=HEADS)
                dve.tensor_reduce(u_max[lane][:, :], s, AX_X, ALU.max).then_inc(u_max_ok[lane], 1)
                dve.wait_ge(u_max_ok[lane], n + 1)
                at_least(dve, u_turned[lane], n)
                tt(u_p[lane][:, :, :], s, u_max[lane][:, :].unsqueeze(2).to_broadcast([P, HEADS, S]), ALU.subtract)\
                    .then_inc(u_sub[lane], 1)

            def normalise(lane, n):
                dve.wait_ge(u_pv[lane], n + 1)
                o = ps_o[lane][:, 0:HEADS * VW].rearrange("p (h v) -> p h v", h=HEADS)
                dve.reciprocal(u_r[lane][:, :], o[:, :, HD]).then_inc(u_r_ok[lane], 1)
                dve.wait_ge(u_r_ok[lane], n + 1)
                at_least(dve, u_oturned[lane], n)
                tt(u_o[lane][:, :].rearrange("p (h d) -> p h d", h=HEADS), o[:, :, 0:HD],
                   u_r[lane][:, :].unsqueeze(2).to_broadcast([P, HEADS, HD]), ALU.mult).then_inc(u_o_ok[lane], 1)

            def modulate(t, turned, count, bank, xs, h, scaled, done, which, used):
                dve.wait_ge(turned, count)
                seqs = bass.ts(t, SEQS)
                view = [P, SEQS, S]
                tt(xs[:, :].rearrange("p (b q) -> p b q", b=SEQS), bank[:, 0:P].rearrange("p (b q) -> p b q", b=SEQS),
                   mod[:, 2 * which, seqs].unsqueeze(2).to_broadcast(view), ALU.mult).then_inc(scaled, 1)
                dve.wait_ge(scaled, count)
                for semaphore, value in used:
                    at_least(dve, semaphore, value)
                tt(h[:, :].rearrange("p (b q) -> p b q", b=SEQS), xs[:, :].rearrange("p (b q) -> p b q", b=SEQS),
                   mod[:, 2 * which + 1, seqs].unsqueeze(2).to_broadcast(view), ALU.add).then_inc(done, 1)

            def z_norm(t, k):
                n = 2 * t + k
                dve.wait_ge(z_ss_ok, n + 1)
                ts(z_ms[:, :], z_ss[:, :], 1.0 / C, RMS_EPS ** 2, ALU.mult, ALU.max).then_inc(z_ms_ok, 1)
                dve.wait_ge(z_rn_ok, n + 1)
                at_least(dve, z_turned, n)
                ts(z_xn[:, :], (z_x, z_x1)[k][:, :], z_rn[:, 0:1], None, ALU.mult).then_inc(z_xn_ok, 1)

            def z_modulate(t, k):
                used = [(z_up, 2 * t)] if k == 0 else [(z_qkv, t + 1)]
                modulate(t, z_turned, 2 * t + k + 1, (g0, g1)[k], z_xs, z_h, z_scaled, z_h_ok, 0, used)

            def z_read_qkv(t):
                dve.wait_ge(z_qkv, t + 1)
                at_least(dve, u_scored[0], use_z(t)[1] - 2)
                for s in range(2):
                    rows = slice(s * P // 2, (s + 1) * P // 2)
                    tt(z_q[rows, s, :].rearrange("p (b q) -> p b q", b=SEQS), g1[rows, 0:P].rearrange("p (b q) -> p b q", b=SEQS),
                       q_scale[rows, bass.ts(t, SEQS)].unsqueeze(2).to_broadcast([P // 2, SEQS, S]), ALU.mult)
                at_least(dve, z_ks_ok, t)
                dve.tensor_copy(z_k[:, :], g1[:, P:2 * P])
                at_least(dve, z_vs_ok, t)
                dve.tensor_copy(z_v[:, :, :, :].rearrange("p b g d -> p (b g d)"), g1[:, 2 * P:3 * P]).then_inc(z_qkv_read, 1)

            def z_residual(t):
                lane, n = use_z(t)
                dve.wait_ge(u_y[lane], n + 1)
                dve.wait_ge(z_xb_ok, t + 1)
                at_least(dve, z_x1b_ok, t)
                tt(z_x1[:, :], ps_o[lane][:, 0:C], z_xb[:, :], ALU.add).then_inc(u_y_read[lane], 1)

            def z_swiglu(t):
                b1 = w("mlp", "b1")
                dve.wait_ge(z_up, 2 * t + 1)
                tt(z_h1[:, :, :], g0[:, :].rearrange("p (c t) -> p c t", c=FC),
                   b1[:, 0:FC].unsqueeze(2).to_broadcast([P, FC, P]), ALU.add).then_inc(z_h1_ok, 1)
                dve.wait_ge(z_up, 2 * t + 2)
                tt(z_h2[:, :, :], g1[:, :].rearrange("p (c t) -> p c t", c=FC),
                   b1[:, FC:].unsqueeze(2).to_broadcast([P, FC, P]), ALU.add).then_inc(z_h2_ok, 1)
                dve.wait_ge(z_th_ok, t + 1)
                stt(z_h1[:, :, :], z_th[:, :, :], 1.0, z_h1[:, :, :], ALU.add, ALU.mult).then_inc(z_act_ok, 1)
                dve.wait_ge(z_act_ok, t + 1)
                dve.wait_ge(z_h2_ok, t + 1)
                at_least(dve, z_down, t)
                tt(z_g[:, :, :], z_h1[:, :, :], z_h2[:, :, :], ALU.mult).then_inc(z_g_ok, 1)

            def z_result(t):
                dve.wait_ge(z_down, t + 1)
                dve.wait_ge(z_x1b_ok, t + 1)
                at_least(dve, a_x_ok, t)
                stt(z_y[:, :], g0[:, 0:C], 0.5, z_x1b[:, :], ALU.mult, ALU.add).then_inc(z_y_ok, 1)

            def layer_norm(t, x_in, st, mv, ve, rs, xn, mv_ok, ve_ok, rs_ok, xn_ok, turned):
                dve.bn_stats(st[:, :], x_in[:, :])
                dve.drain()
                dve.bn_aggr(mv[:, :], st[:, :]).then_inc(mv_ok, 1)
                dve.wait_ge(mv_ok, t + 1)
                ts(ve[:, :], mv[:, 1:2], LN_EPS, None, ALU.add).then_inc(ve_ok, 1)
                dve.wait_ge(rs_ok, t + 1)
                at_least(dve, turned, t)
                ts(xn[:, :], x_in[:, :], mv[:, 0:1], rs[:, 0:1], ALU.subtract, ALU.mult).then_inc(xn_ok, 1)

            def a_norm(t):
                dve.wait_ge(z_y_ok, t + 1)
                layer_norm(t, z_y, a_st, a_mv, a_ve, a_rs, a_xn, a_mv_ok, a_ve_ok, a_rs_ok, a_xn_ok, a_turned)

            def a_modulate(t):
                modulate(t, a_turned, t + 1, g1, a_xs, a_h, a_scaled, a_h_ok, 1, [(a_v_ps, t)])

            def f_norm(t):
                dve.wait_ge(a_x1_ok, t + 1)
                layer_norm(t, f_x, f_st, f_mv, f_ve, f_rs, f_xn, f_mv_ok, f_ve_ok, f_rs_ok, f_xn_ok, f_turned)

            def f_modulate(t):
                modulate(t, f_turned, t + 1, g1, f_xs, f_h, f_scaled, f_h_ok, 2, [(f_up, 2 * t)])

            def a_gate(t, z):
                for m in (2, 3):
                    lane, n = use_a(t, m, z)
                    dve.wait_ge(u_y_read[lane], n + 1)
                logits = a_y[:, :, C:C + M].rearrange("p m j -> p j m")
                dve.tensor_reduce(a_lg[:, :], logits, AX_X, ALU.add).then_inc(a_lg_ok, 1)
                dve.wait_ge(a_lg_ok, t + 1)
                tt(a_lb[:, :], a_lg[:, :], fus_bg, ALU.add).then_inc(a_lb_ok, 1)
                dve.wait_ge(a_lb_ok, t + 1)
                dve.tensor_reduce(a_lm[:, :], a_lb[:, :], AX_X, ALU.max, negate=True).then_inc(a_lm_ok, 1)
                dve.wait_ge(a_le_ok, t + 1)
                dve.reciprocal(a_lr[:, :], a_ls[:, :]).then_inc(a_lr_ok, 1)
                ts(a_f[:, 0, :], a_y[:, 0, 0:C], a_le[:, 0:1], None, ALU.mult).then_inc(a_f_ok, 1)
                for m in range(1, M):
                    dve.wait_ge(a_f_ok, M * t + m)
                    stt(a_f[:, m, :], a_y[:, m, 0:C], a_le[:, m:m + 1], a_f[:, m - 1, :], ALU.mult, ALU.add).then_inc(a_f_ok, 1)
                dve.wait_ge(a_lr_ok, t + 1)
                dve.wait_ge(a_f_ok, M * t + M)
                stt(a_fg[:, :], a_f[:, M - 1, :], a_lr[:, 0:1], gates[:, bass.ds(t, 1), 0:C].rearrange("p o c -> p (o c)"), ALU.mult, ALU.mult).then_inc(a_fg_ok, 1)
                dve.wait_ge(a_fg_ok, t + 1)
                at_least(dve, f_out_ok, t)
                tt(f_x[:, :], a_fg[:, :], a_x[:, :], ALU.add).then_inc(a_x1_ok, 1)

            def f_swiglu(t):
                dve.wait_ge(f_th_ok, t + 1)
                stt(f_v[:, :], f_th[:, :], 1.0, g1[:, :], ALU.add, ALU.mult).then_inc(f_v_ok, 1)
                dve.wait_ge(f_v_ok, t + 1)
                dve.wait_ge(f_up, 2 * t + 2)
                at_least(dve, f_down, t)
                tt(f_g[:, :, :].rearrange("p c t -> p (c t)"), f_v[:, :], g0[:, :], ALU.mult).then_inc(f_g_ok, 1)

            def f_result(t):
                dve.wait_ge(f_down, t + 1)
                stt(f_y[:, :], g0[:, 0:C], 0.5, gates[:, bass.ds(t, 1), C:2 * C].rearrange("p o c -> p (o c)"), ALU.mult, ALU.mult).then_inc(f_y_ok, 1)
                dve.wait_ge(f_y_ok, t + 1)
                at_least(dve, out_stored, 16 * t)
                tt(f_out[:, :], f_y[:, :], f_x[:, :], ALU.add).then_inc(f_out_ok, 1)

            def iteration(i, z=True, f=True):
                if f:
                    f_modulate(i - 1)
                if z:
                    z_norm(i + 1, 0)
                    z_modulate(i + 1, 0)
                if f:
                    f_swiglu(i - 1)
                if z:
                    z_read_qkv(i + 1)
                softmax(*use_a(i, 0, z))
                softmax(*use_a(i, 1, z))
                if f:
                    f_result(i - 1)
                if z:
                    softmax(*use_z(i + 1))
                normalise(*use_a(i, 0, z))
                softmax(*use_a(i, 2, z))
                normalise(*use_a(i, 1, z))
                softmax(*use_a(i, 3, z))
                if z:
                    normalise(*use_z(i + 1))
                    z_residual(i + 1)
                    z_norm(i + 1, 1)
                normalise(*use_a(i, 2, z))
                if z:
                    z_modulate(i + 1, 1)
                normalise(*use_a(i, 3, z))
                if z:
                    z_swiglu(i + 1)
                a_gate(i, z)
                if z:
                    z_result(i + 1)
                    a_norm(i + 1)
                f_norm(i)
                if z:
                    a_modulate(i + 1)

            z_norm(0, 0)
            z_modulate(0, 0)
            z_read_qkv(0)
            softmax(*use_z(0))
            normalise(*use_z(0))
            z_residual(0)
            z_norm(0, 1)
            z_modulate(0, 1)
            dve.wait_ge(in_["mlp"], 16)
            z_swiglu(0)
            z_result(0)
            rest_of_setup()
            a_norm(0)
            a_modulate(0)
            iteration(0, f=False)
            iteration(1)
            with dve.Fori(2, TILES - 1) as i:
                iteration(i)
            iteration(TILES - 1, z=False)
            f_modulate(TILES - 1)
            f_swiglu(TILES - 1)
            f_result(TILES - 1)

        @block.scalar
        def _(act):
            act.wait_ge(in_["cond"], 16)
            act.activation(cond_tanh[:, :], cond_sb[:, :], ACT.Tanh, scale=0.5).then_inc(set_act, 1)
            act.wait_ge(set_pe, 2)
            act.activation(cond_t[:, :], g0[:, 0:B], ACT.Copy, scale=0.5).then_inc(set_act, 1)

            act.wait_ge(set_act, 2)
            act.copy(cond_tok[:, :, :], cond_t[:, :].unsqueeze(2).to_broadcast([P, B, S])).then_inc(set_act, 1)

            def rest_of_setup():
                for m in range(M):
                    act.wait_ge(set_pe, 5 + m)
                    act.copy(wo_fused[:, m, :], g1[:, 0:C + M]).then_inc(set_act, 1)

            def exponential(lane, n):
                act.wait_ge(u_sub[lane], n + 1)
                p = u_p[lane][:, :, :].rearrange("p h k -> p (h k)")
                act.activation(p, p, ACT.Exp).then_inc(u_exp[lane], 1)

            def take_turned(lane, n):
                act.wait_ge(u_turned[lane], n + 1)
                at_least(act, u_pv[lane], n)
                act.copy(u_pt[lane][:, :, :].rearrange("p g t -> p (g t)"), ps_t[lane][:, :]).then_inc(u_pt_ok[lane], 1)

            def take_out(lane, n):
                act.wait_ge(u_oturned[lane], n + 1)
                at_least(act, u_y[lane], n)
                act.copy(u_ot[lane][:, :], ps_o[lane][:, 0:P]).then_inc(u_ot_ok[lane], 1)

            def a_take_y(i, m, z):
                lane, n = use_a(i, m, z)
                act.wait_ge(u_y[lane], n + 1)
                if m == 0:
                    at_least(act, a_f_ok, M * i)
                act.copy(a_y[:, m, :], ps_o[lane][:, 0:C + M]).then_inc(u_y_read[lane], 1)

            def z_square(t, k):
                if k == 0:
                    act.wait_ge(in_x, 16 * t + 16)
                else:
                    act.wait_ge(u_y_read[0], use_z(t)[1] + 1)
                at_least(act, z_ms_ok, 2 * t + k)
                act.activation(z_sq[:, :], (z_x, z_x1)[k][:, :], ACT.Square, accum_out=z_ss[:, :]).then_inc(z_ss_ok, 1)

            def z_tanh(t):
                act.wait_ge(z_h1_ok, t + 1)
                at_least(act, z_act_ok, t)
                act.activation(z_th[:, :, :], z_h1[:, :, :], ACT.Tanh, scale=0.5).then_inc(z_th_ok, 1)

            def a_take_x(t):
                act.wait_ge(z_y_ok, t + 1)
                at_least(act, a_x1_ok, t)
                act.copy(a_x[:, :], z_y[:, :]).then_inc(a_x_ok, 1)

            def a_take_qkv(i):
                act.wait_ge(a_q_ps, i + 1)
                at_least(act, u_scored[0], use_a(i - 1, 3)[1] + 1) if not isinstance(i, int) or i > 0 else None
                q_ps = g0[:, :].rearrange("p (m t) -> p m t", m=M)
                half = P // 2
                act.activation(a_q[0:half, :, 0, :], q_ps[0:half], ACT.Copy, scale=SCALE)
                act.activation(a_q[half:P, :, 1, :], q_ps[half:P], ACT.Copy, scale=SCALE).then_inc(a_q_ok, 1)
                act.wait_ge(a_k_ps, i + 1)
                at_least(act, a_ks_ok, M * i)
                act.copy(a_k[:, :, :].rearrange("p m t -> p (m t)"), g1[:, :]).then_inc(a_k_ok, 1)
                act.wait_ge(a_v_ps, i + 1)
                at_least(act, a_vs_ok, M * i)
                act.copy(a_v[:, :, :, :, :].rearrange("p m b g d -> p (m b g d)"), g0[:, :]).then_inc(a_v_ok, 1)

            def a_gate_exp(t):
                act.wait_ge(a_lm_ok, t + 1)
                at_least(act, a_lr_ok, t)
                act.activation(a_le[:, :], a_lb[:, :], ACT.Exp, bias=a_lm[:, 0:1], accum_out=a_ls[:, :]).then_inc(a_le_ok, 1)

            def f_tanh(t):
                act.wait_ge(f_up, 2 * t + 1)
                at_least(act, f_v_ok, t)
                act.activation(f_th[:, :], g1[:, :], ACT.Tanh, scale=0.5).then_inc(f_th_ok, 1)

            def iteration(i, z=True, f=True):
                a_take_qkv(i)
                if z:
                    z_square(i + 1, 0)
                if f:
                    f_tanh(i - 1)
                exponential(*use_a(i, 0, z))
                exponential(*use_a(i, 1, z))
                take_turned(*use_a(i, 0, z))
                if z:
                    exponential(*use_z(i + 1))
                take_turned(*use_a(i, 1, z))
                exponential(*use_a(i, 2, z))
                take_out(*use_a(i, 0, z))
                if z:
                    take_turned(*use_z(i + 1))
                a_take_y(i, 0, z)
                exponential(*use_a(i, 3, z))
                take_turned(*use_a(i, 2, z))
                take_out(*use_a(i, 1, z))
                if z:
                    take_out(*use_z(i + 1))
                a_take_y(i, 1, z)
                if z:
                    z_square(i + 1, 1)
                take_turned(*use_a(i, 3, z))
                take_out(*use_a(i, 2, z))
                a_take_y(i, 2, z)
                take_out(*use_a(i, 3, z))
                if z:
                    z_tanh(i + 1)
                a_take_y(i, 3, z)
                a_gate_exp(i)
                if z:
                    a_take_x(i + 1)

            z_square(0, 0)
            exponential(*use_z(0))
            take_turned(*use_z(0))
            take_out(*use_z(0))
            z_square(0, 1)
            z_tanh(0)
            rest_of_setup()
            a_take_x(0)
            iteration(0, f=False)
            iteration(1)
            with act.Fori(2, TILES - 1) as i:
                iteration(i)
            iteration(TILES - 1, z=False)
            f_tanh(TILES - 1)

        @block.gpsimd
        def _(pool):
            pool.memset(z_q[:, :, :], 0.0).then_inc(set_pool, 1)
            pool.memset(a_q[:, :, :, :], 0.0).then_inc(set_pool, 1)

            def power(out_, in_, ready, n, done):
                pool.wait_ge(ready, n + 1)
                pool.tensor_tensor(out=out_[:, :], in0=in_[:, :], in1=neg_half[:, :], op=ALU.pow).then_inc(done, 1)

            def spread_keys(k, ks, done):
                for s in range(0, SLOTS, 4):
                    last = pool.tensor_tensor(out=ks[:, s:s + 4, :], in0=k.unsqueeze(1).to_broadcast([P, 4, P]),
                                              in1=slot_mask[:, s:s + 4].unsqueeze(2).to_broadcast([P, 4, P]), op=ALU.mult)
                last.then_inc(done, 1)

            def spread_values(v, vs, done):
                view = [P, SEQS * G, J, HD]
                pool.tensor_tensor(out=vs[:, :, :, :, 0:HD].rearrange("p b g j d -> p (b g) j d"),
                                   in0=v.rearrange("p b g d -> p (b g) d").unsqueeze(2).to_broadcast(view),
                                   in1=j_mask.unsqueeze(1).unsqueeze(3).to_broadcast(view), op=ALU.mult).then_inc(done, 1)

            def a_spread_keys(i, m):
                pool.wait_ge(a_k_ok, i + 1)
                lane, n = use_a(i - 1, m)
                if not isinstance(i, int) or i > 0:
                    pool.wait_ge(u_scored[lane], n + 1)
                spread_keys(a_k[:, m, :], a_ks[:, m, :, :], a_ks_ok)

            def a_spread_values(i, m):
                pool.wait_ge(a_v_ok, i + 1)
                lane, n = use_a(i - 1, m)
                if not isinstance(i, int) or i > 0:
                    pool.wait_ge(u_pv[lane], n + 1)
                spread_values(a_v[:, m, :, :, :], a_vs[:, m, :, :, :, :], a_vs_ok)

            def z_spread(t):
                pool.wait_ge(z_qkv_read, t + 1)
                lane, n = use_z(t - 1) if not isinstance(t, int) or t > 0 else (0, -1)
                at_least(pool, u_scored[lane], n + 1)
                spread_keys(z_k[:, :], z_ks, z_ks_ok)
                at_least(pool, u_pv[lane], n + 1)
                spread_values(z_v[:, :, :, :], z_vs, z_vs_ok)

            def z_add_proj_bias(t):
                pool.wait_ge(in_x, 16 * t + 16)
                lane, n = use_z(t - 1) if not isinstance(t, int) or t > 0 else (0, -1)
                at_least(pool, u_y_read[lane], n + 1)
                pool.tensor_tensor(out=z_xb[:, :], in0=z_x[:, :], in1=packs["rows"][0][:, packs["rows"][1]["proj_b"]], op=ALU.add)\
                    .then_inc(z_xb_ok, 1)

            def z_add_mlp_bias(t):
                lane, n = use_z(t)
                pool.wait_ge(u_y_read[lane], n + 1)
                at_least(pool, z_y_ok, t)
                pool.tensor_tensor(out=z_x1b[:, :], in0=z_x1[:, :], in1=packs["rows"][0][:, packs["rows"][1]["mlp_b2"]], op=ALU.add)\
                    .then_inc(z_x1b_ok, 1)

            def iteration(i, z=True, f=True):
                if z:
                    power(z_rn, z_ms, z_ms_ok, 2 * i + 2, z_rn_ok)
                a_spread_keys(i, 0)
                a_spread_keys(i, 1)
                a_spread_values(i, 0)
                if z:
                    z_spread(i + 1)
                    z_add_proj_bias(i + 1)
                a_spread_values(i, 1)
                a_spread_keys(i, 2)
                a_spread_keys(i, 3)
                a_spread_values(i, 2)
                a_spread_values(i, 3)
                if z:
                    power(z_rn, z_ms, z_ms_ok, 2 * i + 3, z_rn_ok)
                    z_add_mlp_bias(i + 1)
                    power(a_rs, a_ve, a_ve_ok, i + 1, a_rs_ok)
                power(f_rs, f_ve, f_ve_ok, i, f_rs_ok)

            pool.wait_ge(set_dve, 2)
            power(z_rn, z_ms, z_ms_ok, 0, z_rn_ok)
            pool.wait_ge(in_["rows"], 16)
            z_add_proj_bias(0)
            z_spread(0)
            power(z_rn, z_ms, z_ms_ok, 1, z_rn_ok)
            z_add_mlp_bias(0)
            power(a_rs, a_ve, a_ve_ok, 0, a_rs_ok)
            iteration(0, f=False)
            iteration(1)
            with pool.Fori(2, TILES - 1) as i:
                iteration(i)
            iteration(TILES - 1, z=False)


def kernel(**inputs):
    import numpy as np
    import concourse.bacc as bacc
    from concourse.bass_utils import run_bass_kernel_spmd

    a = {k: np.asarray(v) for k, v in inputs.items()}

    def col(v):
        return v.reshape(-1, P).T

    def chunks(m):
        return m.reshape(-1, P, m.shape[1]).transpose(1, 0, 2).reshape(P, -1)

    p = np.arange(P)
    q, k = np.arange(S)[:, None], np.arange(S)[None, :]
    dist = np.abs(q - k)
    bias = [-dist, np.where(dist <= 1, 0.0, -1e9), np.where(q // 2 == k // 2, 0.0, -1e9)]

    def parts(v):
        rest, out = v.astype(np.float32), []
        for _ in range(3):
            part = (rest.view(np.uint32) & np.uint32(0xFFFF0000)).view(np.float32)
            out.append(part)
            rest = rest - part
        return np.concatenate([*out, np.zeros_like(rest)])

    const = {
        "ident": np.eye(P), "same_q": p[:, None] % S == p[None, :] % S, "same_b": p[:, None] // S == p[None, :] // S,
        "key_of": p[:, None] % S == k, "bias": np.concatenate([parts(b) for b in bias], 1),
        "slot_mask": (p[:, None] // HD) % SLOTS == np.arange(SLOTS), "j_mask": p[:, None] // S == np.arange(J),
    }

    def pack(*cols):
        return np.ascontiguousarray(np.concatenate(cols, 1))

    heads = ("grid", "reg", "ent", "sem")
    arrays = {
        "x": a["x"].reshape(-1, C),
        "cond": a["cond_1024"],
        "mask": np.ascontiguousarray(a["mask_BxS_ik0"].reshape(-1, P).T),
        "early": pack(*[const[n].astype(np.float32) for n in ("ident", "same_q", "same_b", "key_of", "bias", "slot_mask", "j_mask")],
                      a["L0_cond_shift_w"].T, a["L0_cond_scale_w"].T,
                      col(a["L0_cond_norm_w"]), col(a["L0_cond_scale_b"]), col(a["L0_cond_shift_b"])),
        "l0": pack(a["L0_cond_qkv_w"].T, a["L0_cond_proj_w"].T),
        "mlp": pack(a["L0_cond_mlp_w1"].T, chunks(a["L0_cond_mlp_w2"].T), col(a["L0_cond_mlp_b1"])),
        "ada": pack(a["L1_cond_ada_w"], col(a["L1_cond_ada_b"]), *[col(a[f"L1_cond_{n}"]) for n in ("ln1_g", "ln1_b", "ln2_g", "ln2_b")],
                    a["L1_cond_fus_wo"], chunks(a["L1_cond_fus_wg"]), *[a[f"L1_cond_{h}_wo"].T for h in heads]),
        "qkv1": pack(*[a[f"L1_cond_{h}_{n}"] for n in ("wq", "wk", "wv") for h in heads]),
        "ffn": pack(a["L1_cond_ffn_w1"], a["L1_cond_ffn_w3"], chunks(a["L1_cond_ffn_w2"])),
        "rows": np.ascontiguousarray(np.concatenate([a["L0_cond_proj_b"], a["L0_cond_mlp_b2"], a["L1_cond_ada_b"][2 * C:3 * C],
                                                     a["L1_cond_ada_b"][5 * C:6 * C], a["L1_cond_fus_bg"]])[None, :]),
    }
    nc = bacc.Bacc("TRN2", target_bir_lowering=False, num_devices=1)
    args = [nc.dram_tensor(f"in_{n}", v.shape, mybir.dt.from_np(v.dtype), kind="ExternalInput").ap() for n, v in arrays.items()]
    out = nc.dram_tensor("out_x", arrays["x"].shape, F32, kind="ExternalOutput").ap()
    build(nc, *args, out)
    r = run_bass_kernel_spmd(nc, [{f"in_{n}": v for n, v in arrays.items()}], core_ids=[0])
    return r.results[0]["out_x"].reshape(a["x"].shape)
```

```python
from contextlib import ExitStack

import concourse.bass as bass
from concourse import mybir

F32 = mybir.dt.float32
BF16 = mybir.dt.bfloat16
ALU = mybir.AluOpType
ACT = mybir.ActivationFunctionType
AX_X = mybir.AxisListType.X

P = 128
S = 32
C = 128
HEADS = 16
HD = C // HEADS
SEQS = P // S
J = 4
G = HEADS // J
SLOTS = 8
M = 4
F = 512
FC = F // P
VW = HD + 1
SCALE = float(HD) ** -0.5
RMS_EPS = 1e-6
LN_EPS = 1e-6
MASKED = 2.0 ** 126

EARLY = {"ident": P, "same_q": P, "same_b": P, "key_of": S, "bias": 3 * S, "slot_mask": SLOTS, "j_mask": J,
         "shift_w": C, "scale_w": C, "norm_w": 1, "scale_b": 1, "shift_b": 1}
L0 = {"qkv": 3 * C, "proj": C}
MLP = {"w1": 2 * F, "w2": F, "b1": 2 * FC}
ADA = {"ada_w": 6 * C, "ada_b": 6, "ln1_g": 1, "ln1_b": 1, "ln2_g": 1, "ln2_b": 1, "fus_wo": C,
       "fus_wg": M * M, "wo_t": M * C}
QKV1 = {"wq": M * C, "wk": M * C, "wv": M * C}
FFN = {"w1": F, "w3": F, "w2": F}
ROWS = {"proj_b": C, "mlp_b2": C, "gate_b": 2 * C, "fus_bg": M}


def columns(layout):
    at, out = 0, {}
    for name, n in layout.items():
        out[name] = slice(at, at + n)
        at += n
    return out, at


def build(nc, x, cond, mask, early, l0, mlp, ada, qkv1, ffn, rows, out):
    TILES = x.shape[0] // P
    B = cond.shape[0]
    STAGES = 3

    with ExitStack() as ctx:
        def sb(name, shape, dt=F32):
            return ctx.enter_context(nc.sbuf_tensor(name, shape, dt))

        def sem(name):
            return ctx.enter_context(nc.semaphore(name))

        def sems(names):
            return [sem(name) for name in names.split()]

        packs = {}
        for name, layout in (("early", EARLY), ("l0", L0), ("mlp", MLP), ("ada", ADA), ("qkv1", QKV1), ("ffn", FFN), ("rows", ROWS)):
            cols, n = columns(layout)
            packs[name] = (sb(f"w_{name}", [P, n]), cols)

        def w(pack, name):
            t, cols = packs[pack]
            return t[:, cols[name]]

        ident = w("early", "ident")
        slot_mask, j_mask = w("early", "slot_mask"), w("early", "j_mask")
        same_q16 = sb("same_q16", [P, P], BF16)
        same_b16 = sb("same_b16", [P, P], BF16)
        bias16 = sb("bias16", [P, 3, S], BF16)
        mask16 = sb("mask16", [P, TILES, S], BF16)
        ones = sb("ones", [P, P])
        neg_half = sb("neg_half", [P, TILES])
        mask_raw = sb("mask_raw", [P, TILES], mybir.dt.int32)
        attended = sb("attended", [P, TILES])
        attended_b = sb("attended_b", [P, TILES, SEQS])
        any_key = sb("any_key", [P, TILES])
        mask_add = sb("mask_add", [P, TILES])
        q_scale = sb("q_scale", [P, B])
        cond_sb = sb("cond_sb", [B, C])
        cond_tanh = sb("cond_tanh", [B, C])
        cond_silu = sb("cond_silu", [B, C])
        cond_t = sb("cond_t", [P, B])
        cond_tok = sb("cond_tok", [P, B, S])
        mod = sb("mod", [P, 6, B])
        scale1 = sb("scale1", [P, B])
        gates = sb("gates", [P, TILES, 2 * C])
        wo_fused = sb("wo_fused", [P, M, C + M])

        x_in = sb("x_in", [P, TILES, C])
        n_sq = sb("n_sq", [P, TILES, C])
        n_ss = sb("n_ss", [P, TILES])
        n_ms = sb("n_ms", [P, TILES])
        n_rn = sb("n_rn", [P, TILES])
        n_xn = sb("n_xn", [P, TILES, C])
        n_xs = sb("n_xs", [P, TILES, P])
        n_h = sb("n_h", [P, TILES, P])
        x_b = sb("x_b", [P, TILES, C])
        x1 = sb("x1", [P, TILES, C])
        x2 = sb("x2", [P, TILES, C])
        x3 = sb("x3", [P, TILES, C])
        x4 = sb("x4", [P, TILES, C])

        z_h = sb("z_h", [P, P])
        z_k = sb("z_k", [P, P])
        z_v = sb("z_v", [P, SEQS, G, HD])
        z_sq = sb("z_sq", [P, C])
        z_ss = sb("z_ss", [P, 1])
        z_ms = sb("z_ms", [P, 1])
        z_rn = sb("z_rn", [P, 1])
        z_xn = sb("z_xn", [P, C])
        z_x1b = sb("z_x1b", [P, C])
        z_xs = sb("z_xs", [P, P])
        z_hm = sb("z_hm", [P, P])
        z_h1 = sb("z_h1", [P, FC, P])
        z_h2 = sb("z_h2", [P, FC, P])
        z_th = sb("z_th", [P, FC, P])
        z_g = sb("z_g", [P, FC, P])
        a_st = sb("a_st", [P, 6])
        a_mv = sb("a_mv", [P, 2])
        a_ve = sb("a_ve", [P, 1])
        a_rs = sb("a_rs", [P, 1])
        a_xn = sb("a_xn", [P, C])
        a_xs = sb("a_xs", [P, P])
        a_h = sb("a_h", [P, P])
        a_k = sb("a_k", [P, M, P])
        a_v = sb("a_v", [P, M, SEQS, G, HD])
        a_y = sb("a_y", [P, M, C + M])
        a_lg = sb("a_lg", [P, M])
        a_lb = sb("a_lb", [P, M])
        a_lm = sb("a_lm", [P, 1])
        a_le = sb("a_le", [P, M])
        a_ls = sb("a_ls", [P, 1])
        a_lr = sb("a_lr", [P, 1])
        a_f = sb("a_f", [P, M, C])
        a_fg = sb("a_fg", [P, C])
        f_st = sb("f_st", [P, 6])
        f_mv = sb("f_mv", [P, 2])
        f_ve = sb("f_ve", [P, 1])
        f_rs = sb("f_rs", [P, 1])
        f_xn = sb("f_xn", [P, C])
        f_xs = sb("f_xs", [P, P])
        f_h = sb("f_h", [P, P])
        f_th = sb("f_th", [P, F])
        f_v = sb("f_v", [P, F])
        f_g = sb("f_g", [P, FC, P])
        f_y = sb("f_y", [P, C])
        UNITS = ("grid", "reg", "ent", "sem", "z")
        Z = M
        qs = sb("qs", [P, M + 1, 2, P])
        ks = sb("ks", [P, M + 1, SLOTS, P])
        vs = sb("vs", [P, M + 1, SEQS, G, J, VW])
        u_max, u_p, u_pt, u_r, u_o, u_ot = (
            [sb(f"{u}_{name}", shape) for u in UNITS] for name, shape in
            (("max", [P, HEADS]), ("p", [P, HEADS, S]), ("pt", [P, G, P]), ("r", [P, HEADS]), ("o", [P, C]), ("ot", [P, P])))

        bank = [ctx.enter_context(nc.psum_tensor(f"bank{n}", [P, 512], F32)) for n in range(8)]
        bank_s, bank_t, bank_o = ([bank[n] for n in banks] for banks in ((2, 4, 5, 0, 2), (1, 7, 5, 6, 7), (3, 4, 6, 1, 5)))
        bank_qkv0, bank_x1, bank_up1, bank_up2, bank_down0 = (bank[n] for n in (1, 3, 4, 7, 0))
        bank_x2, bank_k, bank_q, bank_v = (bank[n] for n in (0, 2, 0, 6))
        bank_x3, bank_w1, bank_w3, bank_down1 = (bank[n] for n in (7, 1, 7, 6))

        bank_c0, bank_c1, bank_n0, bank_n1 = (bank[n] for n in (0, 3, 4, 6))

        in_x, in_x_rest, out_stored = sems("in_x in_x_rest out_stored")
        in_ = {n: sem(f"in_{n}") for n in ("cond", "mask", *packs)}
        set_dve, set_pe, set_act, set_pool, set_chain, set_bank = sems("set_dve set_pe set_act set_pool set_chain set_bank")
        n_ss_ok, n_ms_ok, n_rn_ok, n_xn_ok, n_turned, n_scaled, n_h_ok, x_b_ok = sems(
            "n_ss_ok n_ms_ok n_rn_ok n_xn_ok n_turned n_scaled n_h_ok x_b_ok")
        z_h_ok, z_qkv, z_qkv_read = sems("z_h_ok z_qkv z_qkv_read")
        z_ss_ok, z_ms_ok, z_rn_ok, z_xn_ok, z_xn_turned, z_scaled, z_hm_ok, z_x1b_ok = sems(
            "z_ss_ok z_ms_ok z_rn_ok z_xn_ok z_xn_turned z_scaled z_hm_ok z_x1b_ok")
        z_up1, z_up2, z_h1_ok, z_h2_ok, z_th_ok, z_act_ok, z_g_ok, z_down, x2_ok = sems(
            "z_up1 z_up2 z_h1_ok z_h2_ok z_th_ok z_act_ok z_g_ok z_down x2_ok")
        a_mv_ok, a_ve_ok, a_rs_ok, a_xn_ok, a_turned, a_scaled, a_h_ok = sems(
            "a_mv_ok a_ve_ok a_rs_ok a_xn_ok a_turned a_scaled a_h_ok")
        a_q_ps, a_q_ok, a_k_ps, a_k_ok, a_v_ps, a_v_ok = sems("a_q_ps a_q_ok a_k_ps a_k_ok a_v_ps a_v_ok")
        a_lg_ok, a_lb_ok, a_lm_ok, a_le_ok, a_lr_ok, a_f_ok, a_fg_ok, x3_ok = sems(
            "a_lg_ok a_lb_ok a_lm_ok a_le_ok a_lr_ok a_f_ok a_fg_ok x3_ok")
        f_mv_ok, f_ve_ok, f_rs_ok, f_xn_ok, f_turned, f_scaled, f_h_ok = sems(
            "f_mv_ok f_ve_ok f_rs_ok f_xn_ok f_turned f_scaled f_h_ok")
        f_up1, f_up3, f_th_ok, f_v_ok, f_g_ok, f_down, f_y_ok, x4_ok = sems("f_up1 f_up3 f_th_ok f_v_ok f_g_ok f_down f_y_ok x4_ok")
        ks_ok, vs_ok, scored, max_ok, subtracted, exp_ok, turned, pt_ok, weighed, r_ok, o_ok, o_turned, ot_ok, projected, y_read = (
            sems(" ".join(f"{u}_{name}" for u in UNITS)) for name in
            ("ks_ok", "vs_ok", "scored", "max_ok", "subtracted", "exp_ok", "turned", "pt_ok", "weighed", "r_ok", "o_ok", "o_turned",
             "ot_ok", "projected", "y_read"))

        def made(eng, semaphore, t):
            if not isinstance(t, int) or t >= 0:
                eng.wait_ge(semaphore, t + 1)

        def exists(t):
            return not isinstance(t, int) or 0 <= t < TILES

        def of_tile(buf, t):
            return buf[:, bass.ds(t, 1), :].rearrange("p o c -> p (o c)")

        PARTS = ((0, 1), (1, 4), (4, TILES))

        block = ctx.enter_context(nc.Block())

        @block.sync
        def _(sp):
            def load(name, src):
                sp.dma_start(packs[name][0][:, :], src).then_inc(in_[name], 16)

            sp.dma_start(of_tile(x_in, 0), x[0:P, :]).then_inc(in_x, 16)
            load("early", early)
            sp.dma_start(cond_sb[:, :], cond).then_inc(in_["cond"], 16)
            sp.dma_start(mask_raw[:, :], mask).then_inc(in_["mask"], 16)
            load("l0", l0)
            sp.dma_start(x_in[:, 1:TILES, :], x[P:TILES * P, :].rearrange("(t p) c -> p t c", p=P)).then_inc(in_x_rest, 16)
            sp.dma_start(packs["rows"][0][:, :], rows.to_broadcast([P, rows.shape[1]])).then_inc(in_["rows"], 16)
            load("ada", ada)
            load("mlp", mlp)
            load("qkv1", qkv1)
            load("ffn", ffn)

            def store(t):
                made(sp, x4_ok, t)
                sp.dma_start(out[bass.ts(t, P), :], of_tile(x4, t)).then_inc(out_stored, 16)

            with sp.Fori(0, TILES) as t:
                store(t)
            sp.wait_ge(out_stored, 16 * TILES)

        @block.tensor
        def _(pe):
            mm = pe.matmul

            pe.wait_ge(set_dve, 4)
            pe.wait_ge(in_["early"], 16)
            mm(bank_c0[:, 0:TILES], w("early", "same_b"), attended[:, :], start=True, stop=True)
            mm(bank_c0[:, 32:32 + B], ones[:, :], attended_b[:, :, :], start=True, stop=True).then_inc(set_pe, 1)
            pe.wait_ge(set_dve, 5)
            pe.transpose(bank_c1[:, 0:B], cond_silu[:, :], ident[0:B, 0:B]).then_inc(set_pe, 1)
            pe.wait_ge(set_act, 2)
            mm(bank_c1[:, 32:32 + B], w("early", "shift_w"), cond_t[:, :], start=True, stop=True)
            mm(bank_c1[:, 64:64 + B], w("early", "scale_w"), cond_t[:, :], start=True, stop=True).then_inc(set_pe, 1)
            for n, (first, end) in enumerate(PARTS):
                pe.wait_ge(n_xn_ok, min(n + 1, 2))
                for t in range(first, end):
                    if n == 2:
                        pe.wait_ge(n_h_ok, 1)
                    last = pe.transpose((bank_n0, bank_n1, bank_n0)[n][:, (t - first) * P:(t - first + 1) * P], n_xn[:, t, :], ident)
                last.then_inc(n_turned, 1)
            pe.wait_ge(in_["l0"], 16)

            def rest_of_setup():
                pe.wait_ge(in_["ada"], 16)
                pe.wait_ge(set_dve, 9)
                for n, part in enumerate((0, 1, 3, 4)):
                    last = mm(bank_c0[:, n * B:n * B + B], w("ada", "ada_w")[:, part * C:part * C + C], cond_t[:, :],
                              start=True, stop=True)
                last.then_inc(set_pe, 1)
                for m in range(M):
                    if m > 0:
                        pe.wait_ge(set_act, 3 + m)
                    wo_t = w("ada", "wo_t")[:, m * C:m * C + C]
                    mm(bank_c1[:, 0:C], wo_t, w("ada", "fus_wo"), start=True, stop=True)
                    mm(bank_c1[:, C:C + M], wo_t, w("ada", "fus_wg")[:, m * M:m * M + M], start=True, stop=True).then_inc(set_pe, 1)
                for t in range(TILES):
                    pe.wait_ge(set_dve, 10 + max(t - 1, 0))
                    if t == 1:
                        pe.wait_ge(set_act, 3 + M)
                    per_token = cond_tok[:, SEQS * t:SEQS * t + SEQS, :]
                    g_m, g_f = w("ada", "ada_w")[:, 2 * C:3 * C], w("ada", "ada_w")[:, 5 * C:6 * C]
                    b = (bank_c0, bank_c1)[t % 2]
                    mm(b[:, 0:C], per_token, g_m, start=True, stop=True)
                    mm(b[:, C:2 * C], per_token, g_f, start=True, stop=True).then_inc(set_pe, 1)

            def scores(t, u):
                pe.wait_ge(*( (z_qkv_read, t + 1) if u == Z else (a_q_ok, t + 1)))
                made(pe, ks_ok[u], t)
                b_s = bank_s[u]
                add_w, add = None, None
                if u == Z:
                    add_w, add = same_b16, of_tile(mask16, t)
                elif u < 3:
                    add_w, add = same_q16, bias16[:, u, :]
                if add is not None:
                    mm(b_s[:, :], add_w[:, :], add.unsqueeze(1).to_broadcast([P, HEADS, S]), start=True, stop=False, skip_group_check=True)
                half = SLOTS * S
                for s in range(2):
                    for b in range(SEQS):
                        tok = slice(b * S, b * S + S)
                        last = mm(b_s[tok, s * half:s * half + half], qs[:, u, s, tok], ks[:, u, :, tok],
                                  start=add is None, stop=True, skip_group_check=True)
                last.then_inc(scored[u], 1)

            def turn(t, u):
                made(pe, exp_ok[u], t)
                for g in range(G):
                    last = pe.transpose(bank_t[u][:, g * P:g * P + P], u_p[u][:, g * J:g * J + J, :], ident)
                last.then_inc(turned[u], 1)

            def weigh(t, u):
                made(pe, pt_ok[u], t)
                made(pe, vs_ok[u], t)
                for g in range(G):
                    for b in range(SEQS):
                        tok = slice(b * S, b * S + S)
                        last = mm(bank_o[u][tok, g * J * VW:(g + 1) * J * VW], u_pt[u][:, g, tok],
                                  vs[:, u, b, g, :, :], start=True, stop=True, skip_group_check=True)
                last.then_inc(weighed[u], 1)

            def turn_out(t, u):
                made(pe, o_ok[u], t)
                pe.transpose(bank_o[u][:, 0:P], u_o[u][:, :], ident).then_inc(o_turned[u], 1)

            def project(t, u):
                made(pe, ot_ok[u], t)
                weights = w("l0", "proj") if u == Z else wo_fused[:, u, :]
                mm(bank_o[u][:, 0:weights.shape[1]], u_ot[u][:, :], weights, start=True, stop=True).then_inc(projected[u], 1)

            def z_project(t):
                made(pe, z_h_ok, t)
                b_qkv, qkv = bank_qkv0, w("l0", "qkv")
                mm(b_qkv[:, 0:P], qkv[:, 0:C], z_h[:, :], start=True, stop=True)
                mm(b_qkv[:, P:2 * P], qkv[:, C:2 * C], z_h[:, :], start=True, stop=True)
                wv = qkv[:, 2 * C:].rearrange("c (g j d) -> c g j d", g=G, j=J)
                vw = G * HD
                for b in range(SEQS):
                    for j in range(J):
                        last = mm(b_qkv[j * S:j * S + S, 2 * P + b * vw:2 * P + (b + 1) * vw],
                                  z_h[:, b * S:b * S + S], wv[:, :, j, :], start=True, stop=True, skip_group_check=True)
                last.then_inc(z_qkv, 1)

            def z_turn_x1(t):
                made(pe, z_xn_ok, t)
                pe.transpose(bank_x1[:, 0:P], z_xn[:, :], ident).then_inc(z_xn_turned, 1)

            def up(b, h, weights, done):
                for c in range(FC):
                    last = mm(b[:, c * P:c * P + P], weights[:, c * P:c * P + P], h[:, :], start=True, stop=True)
                last.then_inc(done, 1)

            def down(b, g, weights, done):
                for c in range(FC):
                    last = mm(b[:, 0:C], g[:, c, :], weights[:, c * C:c * C + C], start=c == 0, stop=c == FC - 1)
                last.then_inc(done, 1)

            def z_mlp_up1(t):
                made(pe, z_hm_ok, t)
                up(bank_up1, z_hm, w("mlp", "w1")[:, 0:F], z_up1)

            def z_mlp_up2(t):
                made(pe, z_hm_ok, t)
                up(bank_up2, z_hm, w("mlp", "w1")[:, F:2 * F], z_up2)

            def z_mlp_down(t):
                made(pe, z_g_ok, t)
                down(bank_down0, z_g, w("mlp", "w2"), z_down)

            def a_turn_x2(t):
                made(pe, a_xn_ok, t)
                pe.transpose(bank_x2[:, 0:P], a_xn[:, :], ident).then_inc(a_turned, 1)

            def a_project_k(t):
                made(pe, a_h_ok, t)
                up(bank_k, a_h, w("qkv1", "wk"), a_k_ps)

            def a_project_q(t):
                made(pe, a_h_ok, t)
                up(bank_q, a_h, w("qkv1", "wq"), a_q_ps)

            def a_project_v(t):
                made(pe, a_h_ok, t)
                wv = w("qkv1", "wv").rearrange("c (m g j d) -> c m g j d", m=M, g=G, j=J)
                b_v = bank_v[:, :].rearrange("p (m b v) -> p m b v", m=M, b=SEQS)
                for b in range(SEQS):
                    for j in range(J):
                        last = mm(b_v[j * S:j * S + S, :, b, :], a_h[:, b * S:b * S + S],
                                  wv[:, :, :, j, :].rearrange("c m g d -> c (m g) d"), start=True, stop=True, skip_group_check=True)
                last.then_inc(a_v_ps, 1)

            def f_turn_x3(t):
                made(pe, f_xn_ok, t)
                pe.transpose(bank_x3[:, 0:P], f_xn[:, :], ident).then_inc(f_turned, 1)

            def f_ffn_up1(t):
                made(pe, f_h_ok, t)
                up(bank_w1, f_h, w("ffn", "w1"), f_up1)

            def f_ffn_up3(t):
                made(pe, f_h_ok, t)
                up(bank_w3, f_h, w("ffn", "w3"), f_up3)

            def f_ffn_down(t):
                made(pe, f_g_ok, t)
                down(bank_down1, f_g, w("ffn", "w2"), f_down)

            def run(i, stage, step, *of, after=()):
                if not exists(i - stage):
                    return
                for reader, back in after or ():
                    if exists(i - back):
                        made(pe, reader, i - back)
                        break
                else:
                    if isinstance(i, int) and i > 0 and after:
                        pe.wait_ge(set_dve, 10 + TILES)
                step(i - stage, *of)

            def iteration(i):
                run(i, 0, z_project, after=((f_v_ok, 3), (y_read[3], 3), (pt_ok[0], 3), (z_qkv_read, 1),))
                run(i, 1, z_turn_x1, after=((y_read[0], 3), (z_hm_ok, 2),))
                run(i, 2, scores, 3, after=((a_q_ok, 2), (a_h_ok, 2), (x2_ok, 2), (subtracted[3], 3),))
                run(i, 2, scores, 2, after=((y_read[Z], 1), (pt_ok[2], 3), (subtracted[2], 3),))
                run(i, 1, z_mlp_up1, after=((subtracted[1], 2), (y_read[1], 3), (z_h1_ok, 2),))
                run(i, 2, turn, 0, after=((z_qkv_read, 0), (f_v_ok, 3), (y_read[3], 3), (pt_ok[0], 3),))
                run(i, 1, z_mlp_up2, after=((f_g_ok, 3), (f_h_ok, 3), (pt_ok[Z], 1), (pt_ok[1], 3), (z_h2_ok, 2),))
                run(i, 0, scores, Z, after=((subtracted[0], 2), (a_k_ok, 2), (subtracted[Z], 1),))
                if isinstance(i, int) and i == 0:
                    rest_of_setup()
                run(i, 2, turn, 3, after=((f_y_ok, 3), (a_v_ok, 2), (y_read[2], 3), (pt_ok[3], 3),))
                run(i, 2, weigh, 0, after=((z_hm_ok, 1), (y_read[0], 3),))
                run(i, 2, turn, 2, after=((subtracted[2], 2), (y_read[Z], 1), (pt_ok[2], 3),))
                run(i, 1, z_mlp_down, after=((subtracted[3], 2), (a_q_ok, 2), (a_h_ok, 2), (x2_ok, 2),))
                run(i, 2, turn, 1, after=((z_h2_ok, 1), (f_g_ok, 3), (f_h_ok, 3), (pt_ok[Z], 1), (pt_ok[1], 3),))
                run(i, 2, weigh, 3, after=((pt_ok[0], 2), (z_qkv_read, 0), (f_v_ok, 3), (y_read[3], 3),))
                run(i, 2, weigh, 2, after=((pt_ok[3], 2), (f_y_ok, 3), (a_v_ok, 2), (y_read[2], 3),))
                run(i, 2, weigh, 1, after=((z_h1_ok, 1), (subtracted[1], 2), (y_read[1], 3),))
                run(i, 2, turn_out, 0, after=None)
                run(i, 2, turn_out, 3, after=None)
                run(i, 0, turn, Z, after=((pt_ok[1], 2), (z_h2_ok, 1), (f_g_ok, 3), (f_h_ok, 3), (pt_ok[Z], 1),))
                run(i, 1, a_turn_x2, after=((x2_ok, 1), (subtracted[3], 2), (a_q_ok, 2), (a_h_ok, 2),))
                run(i, 2, turn_out, 2, after=None)
                run(i, 2, project, 0, after=None)
                run(i, 2, turn_out, 1, after=None)
                run(i, 2, project, 3, after=None)
                run(i, 2, project, 2, after=None)
                run(i, 2, project, 1, after=None)
                run(i, 1, a_project_k, after=((subtracted[Z], 0), (subtracted[0], 2), (a_k_ok, 2),))
                run(i, 1, a_project_q, after=((a_h_ok, 1), (x2_ok, 1), (subtracted[3], 2), (a_q_ok, 2),))
                run(i, 0, weigh, Z, after=((pt_ok[2], 2), (subtracted[2], 2), (y_read[Z], 1),))
                run(i, 1, a_project_v, after=((y_read[2], 2), (pt_ok[3], 2), (f_y_ok, 3), (a_v_ok, 2),))
                run(i, 0, turn_out, Z, after=None)
                run(i, 2, f_turn_x3, after=((pt_ok[Z], 0), (pt_ok[1], 2), (z_h2_ok, 1), (f_g_ok, 3), (f_h_ok, 3),))
                run(i, 1, scores, 1, after=((y_read[1], 2), (z_h1_ok, 1), (subtracted[1], 2),))
                run(i, 0, project, Z, after=None)
                run(i, 2, f_ffn_up1, after=((y_read[3], 2), (pt_ok[0], 2), (z_qkv_read, 0), (f_v_ok, 3),))
                run(i, 2, f_ffn_up3, after=((f_h_ok, 2), (pt_ok[Z], 0), (pt_ok[1], 2), (z_h2_ok, 1), (f_g_ok, 3),))
                run(i, 1, scores, 0, after=((a_k_ok, 1), (subtracted[Z], 0), (subtracted[0], 2),))
                run(i, 2, f_ffn_down, after=((a_v_ok, 1), (y_read[2], 2), (pt_ok[3], 2), (f_y_ok, 3),))

            for i in range(STAGES):
                if i == 1:
                    pe.wait_ge(in_["mlp"], 16)
                    pe.wait_ge(in_["qkv1"], 16)
                if i == 2:
                    pe.wait_ge(in_["ffn"], 16)
                iteration(i)
            with pe.Fori(STAGES, TILES) as i:
                iteration(i)
            for i in range(TILES, TILES + STAGES - 1):
                iteration(i)

        @block.vector
        def _(dve):
            tt, ts, stt = dve.tensor_tensor, dve.tensor_scalar, dve.scalar_tensor_tensor
            rows_sb, row_cols = packs["rows"]
            gate_b, fus_bg = rows_sb[:, row_cols["gate_b"]], rows_sb[:, row_cols["fus_bg"]]
            chain = [0]

            def then(ins):
                chain[0] += 1
                ins.then_inc(set_chain, 1)
                dve.wait_ge(set_chain, chain[0])

            dve.memset(ones[:, :], 1.0).then_inc(set_dve, 1)
            dve.memset(neg_half[:, :], -0.5).then_inc(set_dve, 1)
            dve.wait_ge(in_["mask"], 16)
            ts(attended[:, :], mask_raw[:, :], 0.0, None, ALU.not_equal).then_inc(set_dve, 1)
            dve.wait_ge(set_dve, 3)
            dve.wait_ge(in_["early"], 16)
            tt(attended_b[:, :, :], attended[:, :].unsqueeze(2).to_broadcast([P, TILES, SEQS]),
               j_mask.unsqueeze(1).to_broadcast([P, TILES, SEQS]), ALU.mult).then_inc(set_dve, 1)
            dve.wait_ge(set_act, 1)
            stt(cond_silu[:, :], cond_tanh[:, :], 1.0, cond_sb[:, :], ALU.add, ALU.mult).then_inc(set_dve, 1)

            def first_norm(part, first, end):
                dve.wait_ge(n_ss_ok, part + 1)
                ts(n_ms[:, first:end], n_ss[:, first:end], 1.0 / C, RMS_EPS ** 2, ALU.mult, ALU.max).then_inc(n_ms_ok, 1)
                dve.wait_ge(n_rn_ok, part + 1)
                tt(n_xn[:, first:end, :], x_in[:, first:end, :], n_rn[:, first:end].unsqueeze(2).to_broadcast([P, end - first, C]),
                   ALU.mult).then_inc(n_xn_ok, 1)

            def modulate(src, n_seqs, xs, h, scaled, scaled_count, done, which, seqs, used=()):
                view = [P, n_seqs, S]
                tt(xs.rearrange("p (b q) -> p b q", b=n_seqs), src.rearrange("p (b q) -> p b q", b=n_seqs),
                   mod[:, 2 * which, seqs].unsqueeze(2).to_broadcast(view), ALU.mult).then_inc(scaled, 1)
                dve.wait_ge(scaled, scaled_count)
                for semaphore, t in used:
                    made(dve, semaphore, t)
                tt(h.rearrange("p (b q) -> p b q", b=n_seqs), xs.rearrange("p (b q) -> p b q", b=n_seqs),
                   mod[:, 2 * which + 1, seqs].unsqueeze(2).to_broadcast(view), ALU.add).then_inc(done, 1)

            def first_modulate(n):
                first, end = PARTS[n]
                dve.wait_ge(n_turned, n + 1)
                modulate((bank_n0, bank_n1, bank_n0)[n][:, 0:(end - first) * P], (end - first) * SEQS,
                         n_xs[:, first:end, :].rearrange("p t q -> p (t q)"), n_h[:, first:end, :].rearrange("p t q -> p (t q)"),
                         n_scaled, n + 1, n_h_ok, 0, slice(first * SEQS, end * SEQS))

            first_norm(0, 0, 1)
            dve.wait_ge(set_pe, 1)
            ts(any_key[:, :], bank_c0[:, 0:TILES], 1.0, MASKED, ALU.min, ALU.mult).then_inc(set_dve, 1)
            ts(q_scale[:, :], bank_c0[:, 32:32 + B], 1.0, SCALE, ALU.min, ALU.mult).then_inc(set_dve, 1)
            dve.wait_ge(set_dve, 7)
            stt(mask_add[:, :], attended[:, :], 1.0, any_key[:, :], ALU.subtract, ALU.mult).then_inc(set_dve, 1)
            dve.wait_ge(set_dve, 8)
            dve.wait_ge(set_pe, 3)
            ts(mod[:, 1, :], bank_c1[:, 32:32 + B], w("early", "shift_b"), None, ALU.add).then_inc(set_chain, 1)
            chain[0] += 1
            then(ts(scale1[:, :], bank_c1[:, 64:64 + B], w("early", "scale_b"), 1.0, ALU.add, ALU.add))
            then(ts(scale1[:, :], scale1[:, :], 0.1, 10.0, ALU.max, ALU.min))
            then(ts(mod[:, 0, :], scale1[:, :], w("early", "norm_w"), None, ALU.mult))
            first_modulate(0)
            dve.tensor_copy(same_b16[:, :], w("early", "same_b")).then_inc(set_chain, 1)
            chain[0] += 1
            dve.tensor_copy(vs[:, Z, :, :, :, HD].rearrange("p b g j -> p (b g) j"),
                            j_mask.unsqueeze(1).to_broadcast([P, SEQS * G, J])).then_inc(set_chain, 1)
            chain[0] += 1
            dve.wait_ge(set_pool, 1)
            then(tt(mask16[:, :, :], w("early", "key_of").unsqueeze(1).to_broadcast([P, TILES, S]),
                    mask_add[:, :].unsqueeze(2).to_broadcast([P, TILES, S]), ALU.mult))
            first_norm(1, 1, TILES)
            dve.tensor_copy(same_q16[:, :], w("early", "same_q")).then_inc(set_chain, 1)
            dve.tensor_copy(bias16[:, :, :].rearrange("p m k -> p (m k)"), w("early", "bias")).then_inc(set_chain, 1)
            chain[0] += 2
            for m in range(M):
                dve.tensor_copy(vs[:, m, :, :, :, HD].rearrange("p b g j -> p (b g) j"),
                                j_mask.unsqueeze(1).to_broadcast([P, SEQS * G, J])).then_inc(set_chain, 1)
            chain[0] += M
            first_modulate(1)
            first_modulate(2)
            dve.wait_ge(set_chain, chain[0])
            dve.memset(a_lr[:, :], 1.0).then_inc(set_dve, 1)

            def rest_of_setup():
                dve.wait_ge(in_["ada"], 16)
                dve.wait_ge(set_pe, 4)
                for n, (g, b) in enumerate((("ln1_g", "ln1_b"), ("ln2_g", "ln2_b"))):
                    sh, sc = 2 * n, 2 * n + 1
                    part = (0, 1, 3, 4)
                    ada_b = w("ada", "ada_b")
                    then(ts(scale1[:, :], bank_c0[:, sc * B:sc * B + B], ada_b[:, part[sc]:part[sc] + 1], 1.0, ALU.add, ALU.add))
                    then(ts(mod[:, 2 + 2 * n, :], scale1[:, :], w("ada", g), None, ALU.mult))
                    then(ts(mod[:, 3 + 2 * n, :], bank_c0[:, sh * B:sh * B + B], ada_b[:, part[sh]:part[sh] + 1], None, ALU.add))
                    last = stt(mod[:, 3 + 2 * n, :], scale1[:, :], w("ada", b), mod[:, 3 + 2 * n, :], ALU.mult, ALU.add)
                    if n == 0:
                        then(last)
                last.then_inc(set_dve, 1)
                dve.wait_ge(set_dve, 10)
                dve.wait_ge(in_["rows"], 16)
                for t in range(TILES):
                    dve.wait_ge(set_pe, 5 + M + t)
                    tt(gates[:, t, :], (bank_c0, bank_c1)[t % 2][:, 0:2 * C], gate_b, ALU.add).then_inc(set_dve, 1)

            def softmax(t, u):
                made(dve, scored[u], t)
                s = bank_s[u][:, :].rearrange("p (h k) -> p h k", h=HEADS)
                dve.tensor_reduce(u_max[u][:, :], s, AX_X, ALU.max).then_inc(max_ok[u], 1)
                made(dve, max_ok[u], t)
                made(dve, turned[u], t - 1)
                tt(u_p[u][:, :, :], s, u_max[u][:, :].unsqueeze(2).to_broadcast([P, HEADS, S]), ALU.subtract).then_inc(subtracted[u], 1)

            def normalise(t, u):
                made(dve, weighed[u], t)
                o = bank_o[u][:, 0:HEADS * VW].rearrange("p (h v) -> p h v", h=HEADS)
                dve.reciprocal(u_r[u][:, :], o[:, :, HD]).then_inc(r_ok[u], 1)
                made(dve, r_ok[u], t)
                made(dve, o_turned[u], t - 1)
                tt(u_o[u][:, :].rearrange("p (h d) -> p h d", h=HEADS), o[:, :, 0:HD],
                   u_r[u][:, :].unsqueeze(2).to_broadcast([P, HEADS, HD]), ALU.mult).then_inc(o_ok[u], 1)

            def z_read_qkv(t):
                made(dve, z_qkv, t)
                made(dve, scored[Z], t - 1)
                for s in range(2):
                    part = slice(s * P // 2, (s + 1) * P // 2)
                    tt(qs[part, Z, s, :].rearrange("p (b q) -> p b q", b=SEQS), bank_qkv0[part, 0:P].rearrange("p (b q) -> p b q", b=SEQS),
                       q_scale[part, bass.ts(t, SEQS)].unsqueeze(2).to_broadcast([P // 2, SEQS, S]), ALU.mult)
                made(dve, ks_ok[Z], t - 1)
                dve.tensor_copy(z_k[:, :], bank_qkv0[:, P:2 * P])
                made(dve, vs_ok[Z], t - 1)
                dve.tensor_copy(z_v[:, :, :, :].rearrange("p b g d -> p (b g d)"), bank_qkv0[:, 2 * P:3 * P]).then_inc(z_qkv_read, 1)

            def z_residual(t):
                made(dve, projected[Z], t)
                dve.wait_ge(x_b_ok, 1 if isinstance(t, int) and t == 0 else 2)
                tt(of_tile(x1, t), bank_o[Z][:, 0:C], of_tile(x_b, t), ALU.add).then_inc(y_read[Z], 1)

            def z_mean_square(t):
                made(dve, z_ss_ok, t)
                ts(z_ms[:, :], z_ss[:, :], 1.0 / C, RMS_EPS ** 2, ALU.mult, ALU.max).then_inc(z_ms_ok, 1)

            def z_norm(t):
                made(dve, z_rn_ok, t)
                made(dve, z_xn_turned, t - 1)
                ts(z_xn[:, :], of_tile(x1, t), z_rn[:, 0:1], None, ALU.mult).then_inc(z_xn_ok, 1)

            def z_modulate(t):
                made(dve, z_xn_turned, t)
                modulate(bank_x1[:, 0:P], SEQS, z_xs[:, :], z_hm[:, :], z_scaled, t + 1, z_hm_ok, 0, bass.ts(t, SEQS),
                         [(z_up1, t - 1), (z_up2, t - 1)])

            def z_hidden1(t):
                made(dve, z_up1, t)
                made(dve, z_g_ok, t - 1)
                tt(z_h1[:, :, :], bank_up1[:, :].rearrange("p (c t) -> p c t", c=FC),
                   w("mlp", "b1")[:, 0:FC].unsqueeze(2).to_broadcast([P, FC, P]), ALU.add).then_inc(z_h1_ok, 1)

            def z_hidden2(t):
                made(dve, z_up2, t)
                made(dve, z_g_ok, t - 1)
                tt(z_h2[:, :, :], bank_up2[:, :].rearrange("p (c t) -> p c t", c=FC),
                   w("mlp", "b1")[:, FC:].unsqueeze(2).to_broadcast([P, FC, P]), ALU.add).then_inc(z_h2_ok, 1)

            def z_silu(t):
                made(dve, z_th_ok, t)
                stt(z_h1[:, :, :], z_th[:, :, :], 1.0, z_h1[:, :, :], ALU.add, ALU.mult).then_inc(z_act_ok, 1)

            def z_gated(t):
                made(dve, z_act_ok, t)
                made(dve, z_h2_ok, t)
                made(dve, z_down, t - 1)
                tt(z_g[:, :, :], z_h1[:, :, :], z_h2[:, :, :], ALU.mult).then_inc(z_g_ok, 1)

            def z_result(t):
                made(dve, z_down, t)
                made(dve, z_x1b_ok, t)
                stt(of_tile(x2, t), bank_down0[:, 0:C], 0.5, z_x1b[:, :], ALU.mult, ALU.add).then_inc(x2_ok, 1)

            def statistics(t, src, st, mv, ve, mv_ok, ve_ok):
                dve.drain()
                dve.bn_stats(st[:, :], src)
                dve.drain()
                dve.bn_aggr(mv[:, :], st[:, :]).then_inc(mv_ok, 1)
                made(dve, mv_ok, t)
                ts(ve[:, :], mv[:, 1:2], LN_EPS, None, ALU.add).then_inc(ve_ok, 1)

            def a_statistics(t):
                statistics(t, of_tile(x2, t), a_st, a_mv, a_ve, a_mv_ok, a_ve_ok)

            def a_norm(t):
                made(dve, a_rs_ok, t)
                made(dve, a_turned, t - 1)
                ts(a_xn[:, :], of_tile(x2, t), a_mv[:, 0:1], a_rs[:, 0:1], ALU.subtract, ALU.mult).then_inc(a_xn_ok, 1)

            def a_modulate(t):
                made(dve, a_turned, t)
                modulate(bank_x2[:, 0:P], SEQS, a_xs[:, :], a_h[:, :], a_scaled, t + 1, a_h_ok, 1, bass.ts(t, SEQS),
                         [(a_k_ps, t - 1), (a_q_ps, t - 1), (a_v_ps, t - 1)])

            def f_statistics(t):
                statistics(t, of_tile(x3, t), f_st, f_mv, f_ve, f_mv_ok, f_ve_ok)

            def f_norm(t):
                made(dve, f_rs_ok, t)
                made(dve, f_turned, t - 1)
                ts(f_xn[:, :], of_tile(x3, t), f_mv[:, 0:1], f_rs[:, 0:1], ALU.subtract, ALU.mult).then_inc(f_xn_ok, 1)

            def f_modulate(t):
                made(dve, f_turned, t)
                modulate(bank_x3[:, 0:P], SEQS, f_xs[:, :], f_h[:, :], f_scaled, t + 1, f_h_ok, 2, bass.ts(t, SEQS),
                         [(f_up1, t - 1), (f_up3, t - 1)])

            def a_logits(t):
                for m in range(M):
                    made(dve, y_read[m], t)
                logits = a_y[:, :, C:C + M].rearrange("p m j -> p j m")
                dve.tensor_reduce(a_lg[:, :], logits, AX_X, ALU.add).then_inc(a_lg_ok, 1)
                made(dve, a_lg_ok, t)
                tt(a_lb[:, :], a_lg[:, :], fus_bg, ALU.add).then_inc(a_lb_ok, 1)
                made(dve, a_lb_ok, t)
                dve.tensor_reduce(a_lm[:, :], a_lb[:, :], AX_X, ALU.max, negate=True).then_inc(a_lm_ok, 1)

            def a_gate(t):
                made(dve, a_le_ok, t)
                dve.reciprocal(a_lr[:, :], a_ls[:, :]).then_inc(a_lr_ok, 1)
                ts(a_f[:, 0, :], a_y[:, 0, 0:C], a_le[:, 0:1], None, ALU.mult).then_inc(a_f_ok, 1)
                for m in range(1, M):
                    dve.wait_ge(a_f_ok, M * t + m)
                    stt(a_f[:, m, :], a_y[:, m, 0:C], a_le[:, m:m + 1], a_f[:, m - 1, :], ALU.mult, ALU.add).then_inc(a_f_ok, 1)
                made(dve, a_lr_ok, t)
                dve.wait_ge(a_f_ok, M * t + M)
                stt(a_fg[:, :], a_f[:, M - 1, :], a_lr[:, 0:1], of_tile(gates, t)[:, 0:C], ALU.mult, ALU.mult).then_inc(a_fg_ok, 1)
                made(dve, a_fg_ok, t)
                tt(of_tile(x3, t), a_fg[:, :], of_tile(x2, t), ALU.add).then_inc(x3_ok, 1)

            def f_silu(t):
                made(dve, f_th_ok, t)
                made(dve, f_g_ok, t - 1)
                stt(f_v[:, :], f_th[:, :], 1.0, bank_w1[:, :], ALU.add, ALU.mult).then_inc(f_v_ok, 1)

            def f_gated(t):
                made(dve, f_v_ok, t)
                made(dve, f_up3, t)
                made(dve, f_down, t - 1)
                tt(f_g[:, :, :].rearrange("p c t -> p (c t)"), f_v[:, :], bank_w3[:, :], ALU.mult).then_inc(f_g_ok, 1)

            def f_result(t):
                made(dve, f_down, t)
                stt(f_y[:, :], bank_down1[:, 0:C], 0.5, of_tile(gates, t)[:, C:2 * C], ALU.mult, ALU.mult).then_inc(f_y_ok, 1)
                made(dve, f_y_ok, t)
                tt(of_tile(x4, t), f_y[:, :], of_tile(x3, t), ALU.add).then_inc(x4_ok, 1)

            def run(i, stage, step, *of):
                if exists(i - stage):
                    step(i - stage, *of)

            def iteration(i):
                run(i, 0, z_read_qkv)
                run(i, 2, softmax, 3)
                run(i, 2, softmax, 2)
                run(i, 1, z_hidden1)
                run(i, 1, z_silu)
                run(i, 1, z_hidden2)
                run(i, 1, z_gated)
                run(i, 0, softmax, Z)
                if isinstance(i, int) and i == 0:
                    rest_of_setup()
                run(i, 2, normalise, 0)
                run(i, 1, z_result)
                run(i, 1, a_statistics)
                run(i, 2, normalise, 3)
                run(i, 2, normalise, 2)
                run(i, 1, a_norm)
                run(i, 2, normalise, 1)
                run(i, 1, a_modulate)
                run(i, 2, a_logits)
                run(i, 2, a_gate)
                run(i, 2, f_statistics)
                run(i, 0, normalise, Z)
                run(i, 2, f_norm)
                run(i, 2, f_modulate)
                run(i, 0, z_residual)
                run(i, 0, z_mean_square)
                run(i, 1, softmax, 1)
                run(i, 2, f_silu)
                run(i, 0, z_norm)
                run(i, 2, f_gated)
                run(i, 1, softmax, 0)
                run(i, 0, z_modulate)
                run(i, 2, f_result)

            for i in range(STAGES):
                if i == 1:
                    dve.wait_ge(in_["mlp"], 16)
                iteration(i)
            with dve.Fori(STAGES, TILES) as i:
                iteration(i)
            for i in range(TILES, TILES + STAGES - 1):
                iteration(i)

        @block.scalar
        def _(act):
            act.wait_ge(in_["cond"], 16)
            act.activation(cond_tanh[:, :], cond_sb[:, :], ACT.Tanh, scale=0.5).then_inc(set_act, 1)
            act.wait_ge(in_x, 16)
            act.activation(n_sq[:, 0, :], x_in[:, 0, :], ACT.Square, accum_out=n_ss[:, 0:1]).then_inc(n_ss_ok, 1)
            act.wait_ge(set_pe, 2)
            act.activation(cond_t[:, :], bank_c1[:, 0:B], ACT.Copy, scale=0.5).then_inc(set_act, 1)
            act.wait_ge(in_x_rest, 16)
            for t in range(1, TILES):
                last = act.activation(n_sq[:, t, :], x_in[:, t, :], ACT.Square, accum_out=n_ss[:, t:t + 1])
            last.then_inc(n_ss_ok, 1)
            act.wait_ge(set_act, 2)
            act.copy(cond_tok[:, :, :], cond_t[:, :].unsqueeze(2).to_broadcast([P, B, S])).then_inc(set_act, 1)

            def rest_of_setup():
                for m in range(M):
                    act.wait_ge(set_pe, 5 + m)
                    act.copy(wo_fused[:, m, :], bank_c1[:, 0:C + M]).then_inc(set_act, 1)

            def exponential(t, u):
                made(act, subtracted[u], t)
                p = u_p[u][:, :, :].rearrange("p h k -> p (h k)")
                act.activation(p, p, ACT.Exp).then_inc(exp_ok[u], 1)

            def take_turned(t, u):
                made(act, turned[u], t)
                made(act, weighed[u], t - 1)
                act.copy(u_pt[u][:, :, :].rearrange("p g t -> p (g t)"), bank_t[u][:, :]).then_inc(pt_ok[u], 1)

            def take_out(t, u):
                made(act, o_turned[u], t)
                made(act, projected[u], t - 1)
                act.copy(u_ot[u][:, :], bank_o[u][:, 0:P]).then_inc(ot_ok[u], 1)

            def take_y(t, m):
                made(act, projected[m], t)
                made(act, a_fg_ok, t - 1)
                act.copy(a_y[:, m, :], bank_o[m][:, 0:C + M]).then_inc(y_read[m], 1)

            def z_take_h(t):
                act.wait_ge(n_h_ok, 1 + sum(first <= t for first, _ in PARTS[1:]) if isinstance(t, int) else len(PARTS))
                made(act, z_qkv, t - 1)
                act.copy(z_h[:, :], of_tile(n_h, t)).then_inc(z_h_ok, 1)

            def z_square(t):
                made(act, y_read[Z], t)
                made(act, z_ms_ok, t - 1)
                act.activation(z_sq[:, :], of_tile(x1, t), ACT.Square, accum_out=z_ss[:, :]).then_inc(z_ss_ok, 1)

            def z_tanh(t):
                made(act, z_h1_ok, t)
                made(act, z_act_ok, t - 1)
                act.activation(z_th[:, :, :], z_h1[:, :, :], ACT.Tanh, scale=0.5).then_inc(z_th_ok, 1)

            def a_take_q(t):
                made(act, a_q_ps, t)
                for m in range(M):
                    made(act, scored[m], t - 1)
                q_ps = bank_q[:, :].rearrange("p (m t) -> p m t", m=M)
                half = P // 2
                act.activation(qs[0:half, 0:M, 0, :], q_ps[0:half], ACT.Copy, scale=SCALE)
                act.activation(qs[half:P, 0:M, 1, :], q_ps[half:P], ACT.Copy, scale=SCALE).then_inc(a_q_ok, 1)

            def a_take_k(t):
                made(act, a_k_ps, t)
                for m in range(M):
                    made(act, ks_ok[m], t - 1)
                act.copy(a_k[:, :, :].rearrange("p m t -> p (m t)"), bank_k[:, :]).then_inc(a_k_ok, 1)

            def a_take_v(t):
                made(act, a_v_ps, t)
                for m in range(M):
                    made(act, vs_ok[m], t - 1)
                act.copy(a_v[:, :, :, :, :].rearrange("p m b g d -> p (m b g d)"), bank_v[:, :]).then_inc(a_v_ok, 1)

            def a_gate_exp(t):
                made(act, a_lm_ok, t)
                act.activation(a_le[:, :], a_lb[:, :], ACT.Exp, bias=a_lm[:, 0:1], accum_out=a_ls[:, :]).then_inc(a_le_ok, 1)

            def f_tanh(t):
                made(act, f_up1, t)
                made(act, f_v_ok, t - 1)
                act.activation(f_th[:, :], bank_w1[:, :], ACT.Tanh, scale=0.5).then_inc(f_th_ok, 1)

            def run(i, stage, step, *of):
                if exists(i - stage):
                    step(i - stage, *of)

            def iteration(i):
                run(i, 0, z_take_h)
                run(i, 2, a_take_v)
                run(i, 2, exponential, 1)
                run(i, 2, exponential, 0)
                run(i, 2, exponential, 3)
                run(i, 1, z_tanh)
                run(i, 2, take_turned, 0)
                run(i, 2, exponential, 2)
                run(i, 2, take_turned, 3)
                run(i, 2, take_turned, 2)
                run(i, 0, exponential, Z)
                if isinstance(i, int) and i == 0:
                    rest_of_setup()
                run(i, 2, take_turned, 1)
                run(i, 2, take_out, 0)
                run(i, 2, take_out, 3)
                run(i, 2, take_out, 2)
                run(i, 2, take_out, 1)
                run(i, 2, take_y, 3)
                run(i, 2, take_y, 0)
                run(i, 2, take_y, 2)
                run(i, 2, take_y, 1)
                run(i, 2, a_gate_exp)
                run(i, 1, a_take_k)
                run(i, 0, take_turned, Z)
                run(i, 1, a_take_q)
                run(i, 0, take_out, Z)
                run(i, 0, z_square)
                run(i, 2, f_tanh)

            for i in range(STAGES):
                iteration(i)
            with act.Fori(STAGES, TILES) as i:
                iteration(i)
            for i in range(TILES, TILES + STAGES - 1):
                iteration(i)

        @block.gpsimd
        def _(pool):
            tt = pool.tensor_tensor

            pool.memset(qs[:, :, :, :], 0.0).then_inc(set_pool, 1)
            pool.wait_ge(set_dve, 2)

            def first_power(part, first, end):
                pool.wait_ge(n_ms_ok, part + 1)
                tt(out=n_rn[:, first:end], in0=n_ms[:, first:end], in1=neg_half[:, first:end], op=ALU.pow).then_inc(n_rn_ok, 1)

            def add_bias(first, end):
                proj_b = packs["rows"][0][:, packs["rows"][1]["proj_b"]]
                tt(out=x_b[:, first:end, :], in0=x_in[:, first:end, :], in1=proj_b.unsqueeze(1).to_broadcast([P, end - first, C]),
                   op=ALU.add).then_inc(x_b_ok, 1)

            first_power(0, 0, 1)
            first_power(1, 1, TILES)

            def rest_of_setup():
                pool.wait_ge(in_["rows"], 16)
                pool.wait_ge(in_x_rest, 16)
                add_bias(0, 1)
                add_bias(1, TILES)

            def power(t, src, out_, ready, done):
                made(pool, ready, t)
                tt(out=out_[:, :], in0=src[:, :], in1=neg_half[:, 0:1], op=ALU.pow).then_inc(done, 1)

            def spread_keys(t, u, first):
                if first:
                    if u == Z:
                        made(pool, z_qkv_read, t)
                    else:
                        made(pool, a_k_ok, t)
                    made(pool, scored[u], t - 1)
                k = (z_k[:, :] if u == Z else a_k[:, u, :]).unsqueeze(1).to_broadcast([P, SLOTS // 2, P])
                s = slice(0, SLOTS // 2) if first else slice(SLOTS // 2, SLOTS)
                last = tt(out=ks[:, u, s, :], in0=k, in1=slot_mask[:, s].unsqueeze(2).to_broadcast([P, SLOTS // 2, P]), op=ALU.mult)
                if not first:
                    last.then_inc(ks_ok[u], 1)

            def spread_values(t, u):
                if u == Z:
                    made(pool, z_qkv_read, t)
                else:
                    made(pool, a_v_ok, t)
                made(pool, weighed[u], t - 1)
                view = [P, SEQS * G, J, HD]
                v = z_v[:, :, :, :] if u == Z else a_v[:, u, :, :, :]
                tt(out=vs[:, u, :, :, :, 0:HD].rearrange("p b g j d -> p (b g) j d"),
                   in0=v.rearrange("p b g d -> p (b g) d").unsqueeze(2).to_broadcast(view),
                   in1=j_mask.unsqueeze(1).unsqueeze(3).to_broadcast(view), op=ALU.mult).then_inc(vs_ok[u], 1)

            def z_power(t):
                power(t, z_ms, z_rn, z_ms_ok, z_rn_ok)

            def a_power(t):
                power(t, a_ve, a_rs, a_ve_ok, a_rs_ok)

            def f_power(t):
                power(t, f_ve, f_rs, f_ve_ok, f_rs_ok)

            def z_add_mlp_bias(t):
                made(pool, y_read[Z], t)
                made(pool, x2_ok, t - 1)
                tt(out=z_x1b[:, :], in0=of_tile(x1, t), in1=packs["rows"][0][:, packs["rows"][1]["mlp_b2"]], op=ALU.add)\
                    .then_inc(z_x1b_ok, 1)

            def run(i, stage, step, *of):
                if exists(i - stage):
                    step(i - stage, *of)

            def iteration(i):
                run(i, 2, spread_keys, 0, False)
                run(i, 2, spread_keys, 2, True)
                run(i, 1, z_power)
                run(i, 2, spread_keys, 3, False)
                run(i, 2, spread_keys, 2, False)
                run(i, 2, spread_values, 3)
                run(i, 1, z_add_mlp_bias)
                run(i, 0, spread_keys, Z, True)
                run(i, 2, spread_values, 2)
                run(i, 0, spread_keys, Z, False)
                run(i, 2, spread_values, 0)
                run(i, 2, spread_values, 1)
                run(i, 1, a_power)
                run(i, 0, spread_values, Z)
                if isinstance(i, int) and i == 0:
                    rest_of_setup()
                run(i, 1, spread_keys, 1, True)
                run(i, 1, spread_keys, 1, False)
                run(i, 2, f_power)
                run(i, 1, spread_keys, 0, True)
                run(i, 1, spread_keys, 3, True)

            for i in range(STAGES):
                iteration(i)
            with pool.Fori(STAGES, TILES) as i:
                iteration(i)
            for i in range(TILES, TILES + STAGES - 1):
                iteration(i)


def kernel(**inputs):
    import numpy as np
    import concourse.bacc as bacc
    from concourse.bass_utils import run_bass_kernel_spmd

    a = {k: np.asarray(v) for k, v in inputs.items()}

    def col(v):
        return v.reshape(-1, P).T

    def chunks(m):
        return m.reshape(-1, P, m.shape[1]).transpose(1, 0, 2).reshape(P, -1)

    p = np.arange(P)
    q, k = np.arange(S)[:, None], np.arange(S)[None, :]
    dist = np.abs(q - k)
    bias = [-dist, np.where(dist <= 1, 0.0, -1e9), np.where(q // 2 == k // 2, 0.0, -1e9)]

    def parts(v):
        rest, out = v.astype(np.float32), []
        for _ in range(3):
            part = (rest.view(np.uint32) & np.uint32(0xFFFF0000)).view(np.float32)
            out.append(part)
            rest = rest - part
        return np.concatenate([*out, np.zeros_like(rest)])

    const = {
        "ident": np.eye(P), "same_q": p[:, None] % S == p[None, :] % S, "same_b": p[:, None] // S == p[None, :] // S,
        "key_of": p[:, None] % S == k, "bias": np.concatenate([parts(b) for b in bias], 1),
        "slot_mask": (p[:, None] // HD) % SLOTS == np.arange(SLOTS), "j_mask": p[:, None] // S == np.arange(J),
    }

    def pack(*cols):
        return np.ascontiguousarray(np.concatenate(cols, 1))

    heads = ("grid", "reg", "ent", "sem")
    arrays = {
        "x": a["x"].reshape(-1, C),
        "cond": a["cond_1024"],
        "mask": np.ascontiguousarray(a["mask_BxS_ik0"].reshape(-1, P).T),
        "early": pack(*[const[n].astype(np.float32) for n in ("ident", "same_q", "same_b", "key_of", "bias", "slot_mask", "j_mask")],
                      a["L0_cond_shift_w"].T, a["L0_cond_scale_w"].T,
                      col(a["L0_cond_norm_w"]), col(a["L0_cond_scale_b"]), col(a["L0_cond_shift_b"])),
        "l0": pack(a["L0_cond_qkv_w"].T, a["L0_cond_proj_w"].T),
        "mlp": pack(a["L0_cond_mlp_w1"].T, chunks(a["L0_cond_mlp_w2"].T), col(a["L0_cond_mlp_b1"])),
        "ada": pack(a["L1_cond_ada_w"], col(a["L1_cond_ada_b"]), *[col(a[f"L1_cond_{n}"]) for n in ("ln1_g", "ln1_b", "ln2_g", "ln2_b")],
                    a["L1_cond_fus_wo"], chunks(a["L1_cond_fus_wg"]), *[a[f"L1_cond_{h}_wo"].T for h in heads]),
        "qkv1": pack(*[a[f"L1_cond_{h}_{n}"] for n in ("wq", "wk", "wv") for h in heads]),
        "ffn": pack(a["L1_cond_ffn_w1"], a["L1_cond_ffn_w3"], chunks(a["L1_cond_ffn_w2"])),
        "rows": np.ascontiguousarray(np.concatenate([a["L0_cond_proj_b"], a["L0_cond_mlp_b2"], a["L1_cond_ada_b"][2 * C:3 * C],
                                                     a["L1_cond_ada_b"][5 * C:6 * C], a["L1_cond_fus_bg"]])[None, :]),
    }
    nc = bacc.Bacc("TRN2", target_bir_lowering=False, num_devices=1)
    args = [nc.dram_tensor(f"in_{n}", v.shape, mybir.dt.from_np(v.dtype), kind="ExternalInput").ap() for n, v in arrays.items()]
    out = nc.dram_tensor("out_x", arrays["x"].shape, F32, kind="ExternalOutput").ap()
    build(nc, *args, out)
    r = run_bass_kernel_spmd(nc, [{f"in_{n}": v for n, v in arrays.items()}], core_ids=[0])
    return r.results[0]["out_x"].reshape(a["x"].shape)
```

```python
from contextlib import ExitStack

import concourse.bass as bass
from concourse import mybir

F32 = mybir.dt.float32
BF16 = mybir.dt.bfloat16
ALU = mybir.AluOpType
ACT = mybir.ActivationFunctionType
AX_X = mybir.AxisListType.X

P = 128
S = 32
C = 128
HEADS = 16
HD = C // HEADS
SEQS = P // S
J = 4
G = HEADS // J
SLOTS = 8
M = 4
F = 512
FC = F // P
VW = HD + 1
SCALE = float(HD) ** -0.5
RMS_EPS = 1e-6
LN_EPS = 1e-6
MASKED = 2.0 ** 126

EARLY = {"ident": P, "same_q": P, "same_b": P, "key_of": S, "bias": 3 * S, "slot_mask": SLOTS, "j_mask": J,
         "shift_w": C, "scale_w": C, "norm_w": 1, "scale_b": 1, "shift_b": 1}
L0 = {"qkv": 3 * C, "proj": C}
MLP = {"w1": 2 * F, "w2": F, "b1": 2 * FC}
ADA = {"ada_w": 6 * C, "ada_b": 6, "ln1_g": 1, "ln1_b": 1, "ln2_g": 1, "ln2_b": 1, "fus_wo": C,
       "fus_wg": M * M, "wo_t": M * C}
QKV1 = {"wq": M * C, "wk": M * C, "wv": M * C}
FFN = {"w1": F, "w3": F, "w2": F}
ROWS = {"proj_b": C, "mlp_b2": C, "gate_b": 2 * C, "fus_bg": M}


def columns(layout):
    at, out = 0, {}
    for name, n in layout.items():
        out[name] = slice(at, at + n)
        at += n
    return out, at


def build(nc, x, cond, mask, early, l0, mlp, ada, qkv1, ffn, rows, out):
    TILES = x.shape[0] // P
    B = cond.shape[0]
    STAGES = 3

    with ExitStack() as ctx:
        def sb(name, shape, dt=F32):
            return ctx.enter_context(nc.sbuf_tensor(name, shape, dt))

        def sem(name):
            return ctx.enter_context(nc.semaphore(name))

        def sems(names):
            return [sem(name) for name in names.split()]

        packs = {}
        for name, layout in (("early", EARLY), ("l0", L0), ("mlp", MLP), ("ada", ADA), ("qkv1", QKV1), ("ffn", FFN), ("rows", ROWS)):
            cols, n = columns(layout)
            packs[name] = (sb(f"w_{name}", [P, n]), cols)

        def w(pack, name):
            t, cols = packs[pack]
            return t[:, cols[name]]

        ident = w("early", "ident")
        slot_mask, j_mask = w("early", "slot_mask"), w("early", "j_mask")
        same_q16 = sb("same_q16", [P, P], BF16)
        same_b16 = sb("same_b16", [P, P], BF16)
        bias16 = sb("bias16", [P, 3, S], BF16)
        mask16 = sb("mask16", [P, TILES, S], BF16)
        ones = sb("ones", [P, P])
        neg_half = sb("neg_half", [P, TILES])
        mask_raw = sb("mask_raw", [P, TILES], mybir.dt.int32)
        attended = sb("attended", [P, TILES])
        attended_b = sb("attended_b", [P, TILES, SEQS])
        any_key = sb("any_key", [P, TILES])
        mask_add = sb("mask_add", [P, TILES])
        q_scale = sb("q_scale", [P, B])
        cond_sb = sb("cond_sb", [B, C])
        cond_tanh = sb("cond_tanh", [B, C])
        cond_silu = sb("cond_silu", [B, C])
        cond_t = sb("cond_t", [P, B])
        cond_tok = sb("cond_tok", [P, B, S])
        mod = sb("mod", [P, 6, B])
        scale1 = sb("scale1", [P, B])
        gates = sb("gates", [P, TILES, 2 * C])
        wo_fused = sb("wo_fused", [P, M, C + M])

        x_in = sb("x_in", [P, TILES, C])
        n_sq = sb("n_sq", [P, TILES, C])
        n_ss = sb("n_ss", [P, TILES])
        n_ms = sb("n_ms", [P, TILES])
        n_rn = sb("n_rn", [P, TILES])
        n_xn = sb("n_xn", [P, TILES, C])
        n_xs = sb("n_xs", [P, TILES, P])
        n_h = sb("n_h", [P, TILES, P])
        x_b = sb("x_b", [P, TILES, C])
        x1 = sb("x1", [P, TILES, C])
        x2 = sb("x2", [P, TILES, C])
        x3 = sb("x3", [P, TILES, C])
        x4 = sb("x4", [P, TILES, C])

        z_h = sb("z_h", [P, P])
        z_k = sb("z_k", [P, P])
        z_v = sb("z_v", [P, SEQS, G, HD])
        z_sq = sb("z_sq", [P, C])
        z_ss = sb("z_ss", [P, 1])
        z_ms = sb("z_ms", [P, 1])
        z_rn = sb("z_rn", [P, 1])
        z_xn = sb("z_xn", [P, C])
        z_x1b = sb("z_x1b", [P, C])
        z_xs = sb("z_xs", [P, P])
        z_hm = sb("z_hm", [P, P])
        z_h1 = sb("z_h1", [P, FC, P])
        z_act = sb("z_act", [P, FC, P])
        z_th = sb("z_th", [P, FC, P])
        z_g = sb("z_g", [P, FC, P])
        a_st = sb("a_st", [P, 6])
        a_mv = sb("a_mv", [P, 2])
        a_ve = sb("a_ve", [P, 1])
        a_rs = sb("a_rs", [P, 1])
        a_xn = sb("a_xn", [P, C])
        a_xs = sb("a_xs", [P, P])
        a_h = sb("a_h", [P, P])
        a_k = sb("a_k", [P, M, P])
        a_v = sb("a_v", [P, M, SEQS, G, HD])
        a_y = sb("a_y", [P, M, C + M])
        a_lg = sb("a_lg", [P, M])
        a_lb = sb("a_lb", [P, M])
        a_lm = sb("a_lm", [P, 1])
        a_le = sb("a_le", [P, M])
        a_ls = sb("a_ls", [P, 1])
        a_lr = sb("a_lr", [P, 1])
        a_f = sb("a_f", [P, M, C])
        a_fg = sb("a_fg", [P, C])
        f_st = sb("f_st", [P, 6])
        f_mv = sb("f_mv", [P, 2])
        f_ve = sb("f_ve", [P, 1])
        f_rs = sb("f_rs", [P, 1])
        f_xn = sb("f_xn", [P, C])
        f_xs = sb("f_xs", [P, P])
        f_h = sb("f_h", [P, P])
        f_th = sb("f_th", [P, F])
        f_v = sb("f_v", [P, F])
        f_g = sb("f_g", [P, FC, P])
        f_y = sb("f_y", [P, C])
        UNITS = ("grid", "reg", "ent", "sem", "z")
        Z = M
        qs = sb("qs", [P, M + 1, 2, P])
        ks = sb("ks", [P, M + 1, SLOTS, P])
        vs = sb("vs", [P, M + 1, SEQS, G, J, VW])
        u_max, u_p, u_pt, u_r, u_o, u_ot = (
            [sb(f"{u}_{name}", shape) for u in UNITS] for name, shape in
            (("max", [P, HEADS]), ("p", [P, HEADS, S]), ("pt", [P, G, P]), ("r", [P, HEADS]), ("o", [P, C]), ("ot", [P, P])))

        bank = [ctx.enter_context(nc.psum_tensor(f"bank{n}", [P, 512], F32)) for n in range(8)]
        bank_s, bank_t, bank_o = ([bank[n] for n in banks] for banks in ((2, 4, 3, 0, 4), (2, 6, 5, 2, 0), (6, 0, 7, 1, 5)))
        bank_qkv0, bank_x1, bank_up1, bank_up2, bank_down0 = (bank[n] for n in (1, 1, 5, 4, 5))
        bank_x2, bank_k, bank_q, bank_v = (bank[n] for n in (3, 3, 1, 0))
        bank_x3, bank_w1, bank_w3, bank_down1 = (bank[n] for n in (3, 2, 1, 7))

        bank_c0, bank_c1, bank_n0, bank_n1 = (bank[n] for n in (2, 3, 6, 7))
        bank_gates = [(bank_c0, bank_c1)[t % 2] for t in range(TILES)]
        banks_n = bank_n0, bank_n1, bank_n0
        banks_wo = bank_c1, bank_n0, bank_n1, bank_c1

        in_x, in_x_rest, out_stored = sems("in_x in_x_rest out_stored")
        in_ = {n: sem(f"in_{n}") for n in ("cond", "mask", *packs)}
        set_dve, set_pe, set_act, set_pool, set_chain = sems("set_dve set_pe set_act set_pool set_chain")
        n_ss_ok, n_ms_ok, n_rn_ok, n_xn_ok, n_turned, n_scaled, n_h_ok, x_b_ok = sems(
            "n_ss_ok n_ms_ok n_rn_ok n_xn_ok n_turned n_scaled n_h_ok x_b_ok")
        z_h_ok, z_qkv, z_qkv_read, z_kl_ok, a_kl_ok = sems("z_h_ok z_qkv z_qkv_read z_kl_ok a_kl_ok")
        z_ss_ok, z_ms_ok, z_rn_ok, z_xn_ok, z_xn_turned, z_scaled, z_hm_ok, z_x1b_ok = sems(
            "z_ss_ok z_ms_ok z_rn_ok z_xn_ok z_xn_turned z_scaled z_hm_ok z_x1b_ok")
        z_up1, z_up2, z_h1_ok, z_th_ok, z_act_ok, z_g_ok, z_down, x2_ok = sems(
            "z_up1 z_up2 z_h1_ok z_th_ok z_act_ok z_g_ok z_down x2_ok")
        a_mv_ok, a_ve_ok, a_rs_ok, a_xn_ok, a_turned, a_scaled, a_h_ok = sems(
            "a_mv_ok a_ve_ok a_rs_ok a_xn_ok a_turned a_scaled a_h_ok")
        a_q_ps, a_q_ok, a_k_ps, a_k_ok, a_v_ps, a_v_ok = sems("a_q_ps a_q_ok a_k_ps a_k_ok a_v_ps a_v_ok")
        a_lg_ok, a_lb_ok, a_lm_ok, a_le_ok, a_lr_ok, a_f_ok, a_fg_ok, x3_ok = sems(
            "a_lg_ok a_lb_ok a_lm_ok a_le_ok a_lr_ok a_f_ok a_fg_ok x3_ok")
        f_mv_ok, f_ve_ok, f_rs_ok, f_xn_ok, f_turned, f_scaled, f_h_ok = sems(
            "f_mv_ok f_ve_ok f_rs_ok f_xn_ok f_turned f_scaled f_h_ok")
        f_up1, f_up3, f_th_ok, f_v_ok, f_g_ok, f_down, f_y_ok, x4_ok = sems("f_up1 f_up3 f_th_ok f_v_ok f_g_ok f_down f_y_ok x4_ok")
        ks_ok, vs_ok, scored, max_ok, subtracted, exp_ok, turned, pt_ok, weighed, r_ok, o_ok, o_turned, ot_ok, projected, y_read = (
            sems(" ".join(f"{u}_{name}" for u in UNITS)) for name in
            ("ks_ok", "vs_ok", "scored", "max_ok", "subtracted", "exp_ok", "turned", "pt_ok", "weighed", "r_ok", "o_ok", "o_turned",
             "ot_ok", "projected", "y_read"))

        def made(eng, semaphore, t):
            if not isinstance(t, int) or t >= 0:
                eng.wait_ge(semaphore, t + 1)

        def exists(t):
            return not isinstance(t, int) or 0 <= t < TILES

        def at(i, n):
            return isinstance(i, int) and i == n

        def loaded(eng, name, t):
            if isinstance(t, int) and t == 0:
                eng.wait_ge(in_[name], 16)

        def of_tile(buf, t):
            return buf[:, bass.ds(t, 1), :].rearrange("p o c -> p (o c)")

        PARTS = ((0, 1), (1, 4), (4, TILES))

        block = ctx.enter_context(nc.Block())

        @block.sync
        def _(sp):
            def load(name, src):
                sp.dma_start(packs[name][0][:, :], src).then_inc(in_[name], 16)

            sp.dma_start(of_tile(x_in, 0), x[0:P, :]).then_inc(in_x, 16)
            load("early", early)
            sp.dma_start(cond_sb[:, :], cond).then_inc(in_["cond"], 16)
            sp.dma_start(mask_raw[:, :], mask).then_inc(in_["mask"], 16)
            load("l0", l0)
            sp.dma_start(x_in[:, 1:TILES, :], x[P:TILES * P, :].rearrange("(t p) c -> p t c", p=P)).then_inc(in_x_rest, 16)
            sp.dma_start(packs["rows"][0][:, :], rows.to_broadcast([P, rows.shape[1]])).then_inc(in_["rows"], 16)
            load("ada", ada)
            load("mlp", mlp)
            load("qkv1", qkv1)
            load("ffn", ffn)

            def store(t):
                made(sp, x4_ok, t)
                sp.dma_start(out[bass.ts(t, P), :], of_tile(x4, t)).then_inc(out_stored, 16)

            with sp.Fori(0, TILES) as t:
                store(t)
            sp.wait_ge(out_stored, 16 * TILES)

        @block.tensor
        def _(pe):
            mm = pe.matmul

            def keep_busy(n, idle=bank_n1):
                for _ in range(n):
                    mm(idle[:, 0:P], ones[:, :], ones[:, :], start=True, stop=True)

            pe.wait_ge(set_dve, 1)
            keep_busy(9)

            pe.wait_ge(set_dve, 4)
            pe.wait_ge(in_["early"], 16)
            mm(bank_c0[:, 0:TILES], w("early", "same_b"), attended[:, :], start=True, stop=True)
            mm(bank_c0[:, 32:32 + B], ones[:, :], attended_b[:, :, :], start=True, stop=True).then_inc(set_pe, 1)
            pe.wait_ge(set_dve, 5)
            pe.transpose(bank_c1[:, 0:B], cond_silu[:, :], ident[0:B, 0:B]).then_inc(set_pe, 1)
            pe.wait_ge(set_act, 2)
            mm(bank_c1[:, 32:32 + B], w("early", "shift_w"), cond_t[:, :], start=True, stop=True)
            mm(bank_c1[:, 64:64 + B], w("early", "scale_w"), cond_t[:, :], start=True, stop=True).then_inc(set_pe, 1)

            def turn_first_norm(n):
                begin, end = PARTS[n]
                pe.wait_ge(n_xn_ok, min(n + 1, 2))
                for t in range(begin, end):
                    last = pe.transpose(banks_n[n][:, (t - begin) * P:(t - begin + 1) * P], n_xn[:, t, :], ident)
                last.then_inc(n_turned, 1)

            turn_first_norm(0)
            keep_busy(5)
            pe.wait_ge(in_["l0"], 16)

            def setup_ada():
                pe.wait_ge(in_["ada"], 16)
                pe.wait_ge(set_dve, 9)
                for n, part in enumerate((0, 1, 3, 4)):
                    last = mm(bank_c0[:, n * B:n * B + B], w("ada", "ada_w")[:, part * C:part * C + C], cond_t[:, :],
                              start=True, stop=True)
                last.then_inc(set_pe, 1)
                pe.wait_ge(n_h_ok, 1)

            def setup_fused(part):
                for m in part:
                    if m == 3:
                        pe.wait_ge(set_act, 4)
                    wo_t = w("ada", "wo_t")[:, m * C:m * C + C]
                    mm(banks_wo[m][:, 0:C], wo_t, w("ada", "fus_wo"), start=True, stop=True)
                    mm(banks_wo[m][:, C:C + M], wo_t, w("ada", "fus_wg")[:, m * M:m * M + M], start=True, stop=True).then_inc(set_pe, 1)

            def setup_first_norm():
                pe.wait_ge(set_act, 3 + M)
                turn_first_norm(1)
                turn_first_norm(2)

            def setup_gates(tiles):
                for t in tiles:
                    pe.wait_ge(set_dve, 10 + max(t - 1, 0))
                    if t == 1:
                        pe.wait_ge(set_act, 3 + M)
                    per_token = cond_tok[:, SEQS * t:SEQS * t + SEQS, :]
                    g_m, g_f = w("ada", "ada_w")[:, 2 * C:3 * C], w("ada", "ada_w")[:, 5 * C:6 * C]
                    b = bank_gates[t]
                    mm(b[:, 0:C], per_token, g_m, start=True, stop=True)
                    mm(b[:, C:2 * C], per_token, g_f, start=True, stop=True).then_inc(set_pe, 1)

            def scores(t, u):
                pe.wait_ge(*( (z_qkv_read, t + 1) if u == Z else (a_q_ok, t + 1)))
                made(pe, z_kl_ok if u == Z else a_kl_ok, t)
                made(pe, ks_ok[u], t)
                b_s = bank_s[u]
                add_w, add = None, None
                if u == Z:
                    add_w, add = same_b16, of_tile(mask16, t)
                elif u < 3:
                    add_w, add = same_q16, bias16[:, u, :]
                if add is not None:
                    mm(b_s[:, :], add_w[:, :], add.unsqueeze(1).to_broadcast([P, HEADS, S]), start=True, stop=False, skip_group_check=True)
                half = SLOTS * S
                for s in range(2):
                    for b in range(SEQS):
                        tok = slice(b * S, b * S + S)
                        last = mm(b_s[tok, s * half:s * half + half], qs[:, u, s, tok], ks[:, u, :, tok],
                                  start=add is None, stop=True, skip_group_check=True)
                last.then_inc(scored[u], 1)

            def turn(t, u):
                made(pe, exp_ok[u], t)
                for g in range(G):
                    last = pe.transpose(bank_t[u][:, g * P:g * P + P], u_p[u][:, g * J:g * J + J, :], ident)
                last.then_inc(turned[u], 1)

            def weigh(t, u):
                made(pe, pt_ok[u], t)
                made(pe, vs_ok[u], t)
                for g in range(G):
                    for b in range(SEQS):
                        tok = slice(b * S, b * S + S)
                        last = mm(bank_o[u][tok, g * J * VW:(g + 1) * J * VW], u_pt[u][:, g, tok],
                                  vs[:, u, b, g, :, :], start=True, stop=True, skip_group_check=True)
                last.then_inc(weighed[u], 1)

            def turn_out(t, u):
                made(pe, o_ok[u], t)
                pe.transpose(bank_o[u][:, 0:P], u_o[u][:, :], ident).then_inc(o_turned[u], 1)

            def project(t, u):
                made(pe, ot_ok[u], t)
                weights = w("l0", "proj") if u == Z else wo_fused[:, u, :]
                mm(bank_o[u][:, 0:weights.shape[1]], u_ot[u][:, :], weights, start=True, stop=True).then_inc(projected[u], 1)

            def z_project(t):
                made(pe, z_h_ok, t)
                b_qkv, qkv = bank_qkv0, w("l0", "qkv")
                mm(b_qkv[:, 0:P], qkv[:, 0:C], z_h[:, :], start=True, stop=True)
                mm(b_qkv[:, P:2 * P], qkv[:, C:2 * C], z_h[:, :], start=True, stop=True)
                wv = qkv[:, 2 * C:].rearrange("c (g j d) -> c g j d", g=G, j=J)
                vw = G * HD
                for b in range(SEQS):
                    for j in range(J):
                        last = mm(b_qkv[j * S:j * S + S, 2 * P + b * vw:2 * P + (b + 1) * vw],
                                  z_h[:, b * S:b * S + S], wv[:, :, j, :], start=True, stop=True, skip_group_check=True)
                last.then_inc(z_qkv, 1)

            def z_turn_x1(t):
                made(pe, z_xn_ok, t)
                pe.transpose(bank_x1[:, 0:P], z_xn[:, :], ident).then_inc(z_xn_turned, 1)

            def up(b, h, weights, done):
                for c in range(FC):
                    last = mm(b[:, c * P:c * P + P], weights[:, c * P:c * P + P], h[:, :], start=True, stop=True)
                last.then_inc(done, 1)

            def down(b, g, weights, done):
                for c in range(FC):
                    last = mm(b[:, 0:C], g[:, c, :], weights[:, c * C:c * C + C], start=c == 0, stop=c == FC - 1)
                last.then_inc(done, 1)

            def z_mlp_up1(t):
                loaded(pe, "mlp", t)
                made(pe, z_hm_ok, t)
                up(bank_up1, z_hm, w("mlp", "w1")[:, 0:F], z_up1)

            def z_mlp_up2(t):
                loaded(pe, "mlp", t)
                made(pe, z_hm_ok, t)
                up(bank_up2, z_hm, w("mlp", "w1")[:, F:2 * F], z_up2)

            def z_mlp_down(t):
                made(pe, z_g_ok, t)
                down(bank_down0, z_g, w("mlp", "w2"), z_down)

            def a_turn_x2(t):
                made(pe, a_xn_ok, t)
                pe.transpose(bank_x2[:, 0:P], a_xn[:, :], ident).then_inc(a_turned, 1)

            def a_project_k(t):
                loaded(pe, "qkv1", t)
                made(pe, a_h_ok, t)
                up(bank_k, a_h, w("qkv1", "wk"), a_k_ps)

            def a_project_q(t):
                loaded(pe, "qkv1", t)
                made(pe, a_h_ok, t)
                up(bank_q, a_h, w("qkv1", "wq"), a_q_ps)

            def a_project_v(t):
                loaded(pe, "qkv1", t)
                made(pe, a_h_ok, t)
                wv = w("qkv1", "wv").rearrange("c (m g j d) -> c m g j d", m=M, g=G, j=J)
                b_v = bank_v[:, :].rearrange("p (m b v) -> p m b v", m=M, b=SEQS)
                for b in range(SEQS):
                    for j in range(J):
                        last = mm(b_v[j * S:j * S + S, :, b, :], a_h[:, b * S:b * S + S],
                                  wv[:, :, :, j, :].rearrange("c m g d -> c (m g) d"), start=True, stop=True, skip_group_check=True)
                last.then_inc(a_v_ps, 1)

            def f_turn_x3(t):
                if isinstance(t, int) and t == TILES - 1:
                    keep_busy(18, bank_x3)
                made(pe, f_xn_ok, t)
                pe.transpose(bank_x3[:, 0:P], f_xn[:, :], ident).then_inc(f_turned, 1)

            def f_ffn_up1(t):
                loaded(pe, "ffn", t)
                made(pe, f_h_ok, t)
                up(bank_w1, f_h, w("ffn", "w1"), f_up1)

            def f_ffn_up3(t):
                loaded(pe, "ffn", t)
                made(pe, f_h_ok, t)
                up(bank_w3, f_h, w("ffn", "w3"), f_up3)

            def f_ffn_down(t):
                made(pe, f_g_ok, t)
                down(bank_down1, f_g, w("ffn", "w2"), f_down)

            read_c0 = read_c1 = (set_dve, 10 + TILES)
            read_n0, read_n1 = (n_h_ok, len(PARTS)), (n_h_ok, 2)

            def run(i, stage, step, *of, after=(), setup=None):
                if not exists(i - stage):
                    return
                for reader, back in after:
                    if exists(i - back):
                        made(pe, reader, i - back)
                        break
                else:
                    if setup and isinstance(i, int):
                        pe.wait_ge(*setup)
                step(i - stage, *of)

            def iteration(i):
                run(i, 2, turn, 2, after=((z_h1_ok, 1), (x2_ok, 2),))
                run(i, 0, z_project, after=((f_g_ok, 3), (z_hm_ok, 1),))
                if at(i, 0):
                    setup_ada()
                    setup_fused(range(M - 1))
                run(i, 2, weigh, 1, after=((subtracted[3], 2),))
                run(i, 2, turn, 3, after=((pt_ok[0], 2),), setup=read_c1)
                run(i, 1, z_mlp_down, after=((pt_ok[2], 2), (z_h1_ok, 1),))
                if at(i, 1):
                    setup_gates((7,))
                run(i, 2, weigh, 0, after=((pt_ok[1], 2),), setup=read_n1)
                run(i, 2, weigh, 2, after=((f_y_ok, 3),), setup=read_c0)
                run(i, 2, weigh, 3, after=((z_qkv_read, 0), (f_g_ok, 3),))
                run(i, 2, turn_out, 1)
                run(i, 0, scores, Z, after=((z_g_ok, 1),))
                if at(i, 0):
                    setup_fused((M - 1,))
                    setup_gates((0, 1))
                run(i, 2, turn_out, 0)
                run(i, 2, turn_out, 2)
                run(i, 2, project, 1)
                run(i, 2, turn_out, 3)
                run(i, 2, project, 0)
                run(i, 1, a_turn_x2, after=((subtracted[2], 2),), setup=read_n0)
                run(i, 2, project, 2)
                run(i, 2, project, 3)
                run(i, 1, a_project_k, after=((a_h_ok, 1),), setup=read_n0)
                run(i, 0, turn, Z, after=((y_read[1], 2), (pt_ok[Z], 1),))
                run(i, 1, a_project_q, after=((y_read[3], 2), (z_qkv_read, 0),))
                run(i, 0, weigh, Z, after=((x2_ok, 1),))
                if at(i, 0):
                    setup_first_norm()
                run(i, 1, a_project_v, after=((pt_ok[Z], 0), (y_read[1], 2),))
                run(i, 0, turn_out, Z)
                if at(i, 0):
                    setup_gates((2,))
                run(i, 0, project, Z)
                if at(i, 0):
                    setup_gates((3, 4,))
                run(i, 2, f_turn_x3, after=((a_kl_ok, 1), (subtracted[2], 2),), setup=read_n0)
                run(i, 1, scores, 0, after=((pt_ok[3], 2),), setup=read_c1)
                run(i, 1, scores, 1, after=((subtracted[Z], 0), (z_g_ok, 1),))
                run(i, 0, z_turn_x1, after=((a_q_ok, 1), (z_qkv_read, 0),))
                run(i, 1, scores, 2, after=((f_h_ok, 2), (a_kl_ok, 1),), setup=read_n0)
                run(i, 0, z_mlp_up1, after=((y_read[Z], 0),))
                run(i, 2, f_ffn_up1, after=((subtracted[0], 1), (pt_ok[3], 2),), setup=read_c1)
                run(i, 2, f_ffn_up3, after=((z_hm_ok, 0), (a_q_ok, 1), (y_read[3], 2),))
                run(i, 1, scores, 3, after=((a_v_ok, 1),))
                run(i, 0, z_mlp_up2, after=((subtracted[1], 1), (subtracted[Z], 0),))
                if at(i, 0):
                    setup_gates((5,6,))
                run(i, 1, turn, 0, after=((f_v_ok, 2), (subtracted[0], 1),), setup=read_c1)
                run(i, 1, turn, 1, after=((y_read[0], 2),), setup=read_n1)
                run(i, 2, f_ffn_down, after=((y_read[2], 2),), setup=read_c0)

            for i in range(STAGES):
                iteration(i)
            with pe.Fori(STAGES, TILES) as i:
                iteration(i)
            for i in range(TILES, TILES + STAGES - 1):
                iteration(i)

        @block.vector
        def _(dve):
            tt, ts, stt = dve.tensor_tensor, dve.tensor_scalar, dve.scalar_tensor_tensor
            rows_sb, row_cols = packs["rows"]
            gate_b, fus_bg = rows_sb[:, row_cols["gate_b"]], rows_sb[:, row_cols["fus_bg"]]
            chain = [0]

            def then(ins):
                chain[0] += 1
                ins.then_inc(set_chain, 1)
                dve.wait_ge(set_chain, chain[0])

            dve.memset(ones[:, :], 1.0).then_inc(set_dve, 1)
            dve.memset(neg_half[:, :], -0.5).then_inc(set_dve, 1)
            dve.wait_ge(in_["mask"], 16)
            ts(attended[:, :], mask_raw[:, :], 0.0, None, ALU.not_equal).then_inc(set_dve, 1)
            dve.wait_ge(set_dve, 3)
            dve.wait_ge(in_["early"], 16)
            tt(attended_b[:, :, :], attended[:, :].unsqueeze(2).to_broadcast([P, TILES, SEQS]),
               j_mask.unsqueeze(1).to_broadcast([P, TILES, SEQS]), ALU.mult).then_inc(set_dve, 1)
            dve.wait_ge(set_act, 1)
            stt(cond_silu[:, :], cond_tanh[:, :], 1.0, cond_sb[:, :], ALU.add, ALU.mult).then_inc(set_dve, 1)

            def first_mean_square(part, begin, end):
                dve.wait_ge(n_ss_ok, part + 1)
                ts(n_ms[:, begin:end], n_ss[:, begin:end], 1.0 / C, RMS_EPS ** 2, ALU.mult, ALU.max).then_inc(n_ms_ok, 1)

            def first_norm(part, begin, end):
                dve.wait_ge(n_rn_ok, part + 1)
                tt(n_xn[:, begin:end, :], x_in[:, begin:end, :], n_rn[:, begin:end].unsqueeze(2).to_broadcast([P, end - begin, C]),
                   ALU.mult).then_inc(n_xn_ok, 1)

            def modulate(src, n_seqs, xs, h, scaled, scaled_count, done, which, seqs, used=()):
                view = [P, n_seqs, S]
                tt(xs.rearrange("p (b q) -> p b q", b=n_seqs), src.rearrange("p (b q) -> p b q", b=n_seqs),
                   mod[:, 2 * which, seqs].unsqueeze(2).to_broadcast(view), ALU.mult).then_inc(scaled, 1)
                dve.wait_ge(scaled, scaled_count)
                for semaphore, t in used:
                    made(dve, semaphore, t)
                tt(h.rearrange("p (b q) -> p b q", b=n_seqs), xs.rearrange("p (b q) -> p b q", b=n_seqs),
                   mod[:, 2 * which + 1, seqs].unsqueeze(2).to_broadcast(view), ALU.add).then_inc(done, 1)

            def first_modulate(n):
                begin, end = PARTS[n]
                dve.wait_ge(n_turned, n + 1)
                modulate(banks_n[n][:, 0:(end - begin) * P], (end - begin) * SEQS,
                         n_xs[:, begin:end, :].rearrange("p t q -> p (t q)"), n_h[:, begin:end, :].rearrange("p t q -> p (t q)"),
                         n_scaled, n + 1, n_h_ok, 0, slice(begin * SEQS, end * SEQS))

            first_mean_square(0, 0, 1)
            first_norm(0, 0, 1)
            dve.wait_ge(set_pe, 1)
            ts(any_key[:, :], bank_c0[:, 0:TILES], 1.0, MASKED, ALU.min, ALU.mult).then_inc(set_dve, 1)
            ts(q_scale[:, :], bank_c0[:, 32:32 + B], 1.0, SCALE, ALU.min, ALU.mult).then_inc(set_dve, 1)
            dve.wait_ge(set_dve, 7)
            stt(mask_add[:, :], attended[:, :], 1.0, any_key[:, :], ALU.subtract, ALU.mult).then_inc(set_dve, 1)
            dve.tensor_copy(same_b16[:, :], w("early", "same_b")).then_inc(set_chain, 1)
            dve.tensor_copy(same_q16[:, :], w("early", "same_q")).then_inc(set_chain, 1)
            dve.tensor_copy(bias16[:, :, :].rearrange("p m k -> p (m k)"), w("early", "bias")).then_inc(set_chain, 1)
            for u in range(M + 1):
                dve.tensor_copy(vs[:, u, :, :, :, HD].rearrange("p b g j -> p (b g) j"),
                                j_mask.unsqueeze(1).to_broadcast([P, SEQS * G, J])).then_inc(set_chain, 1)
            chain[0] += 3 + M + 1
            dve.wait_ge(set_dve, 8)
            dve.wait_ge(set_chain, chain[0])
            tt(mask16[:, :, :], w("early", "key_of").unsqueeze(1).to_broadcast([P, TILES, S]),
               mask_add[:, :].unsqueeze(2).to_broadcast([P, TILES, S]), ALU.mult).then_inc(set_dve, 1)
            dve.wait_ge(set_pe, 3)
            ts(mod[:, 1, :], bank_c1[:, 32:32 + B], w("early", "shift_b"), None, ALU.add).then_inc(set_chain, 1)
            chain[0] += 1
            then(ts(scale1[:, :], bank_c1[:, 64:64 + B], w("early", "scale_b"), 1.0, ALU.add, ALU.add))
            then(ts(scale1[:, :], scale1[:, :], 0.1, 10.0, ALU.max, ALU.min))
            then(ts(mod[:, 0, :], scale1[:, :], w("early", "norm_w"), None, ALU.mult))
            first_modulate(0)
            dve.wait_ge(set_pool, 1)
            dve.wait_ge(set_dve, 9)

            def setup_ada():
                dve.wait_ge(in_["ada"], 16)
                dve.wait_ge(set_pe, 4)
                for n, (g, b) in enumerate((("ln1_g", "ln1_b"), ("ln2_g", "ln2_b"))):
                    sh, sc = 2 * n, 2 * n + 1
                    part = (0, 1, 3, 4)
                    ada_b = w("ada", "ada_b")
                    then(ts(scale1[:, :], bank_c0[:, sc * B:sc * B + B], ada_b[:, part[sc]:part[sc] + 1], 1.0, ALU.add, ALU.add))
                    then(ts(mod[:, 2 + 2 * n, :], scale1[:, :], w("ada", g), None, ALU.mult))
                    then(ts(mod[:, 3 + 2 * n, :], bank_c0[:, sh * B:sh * B + B], ada_b[:, part[sh]:part[sh] + 1], None, ALU.add))
                    last = stt(mod[:, 3 + 2 * n, :], scale1[:, :], w("ada", b), mod[:, 3 + 2 * n, :], ALU.mult, ALU.add)
                    if n == 0:
                        then(last)
                last.then_inc(set_dve, 1)
                dve.wait_ge(set_dve, 10)

            def setup_gates(tiles):
                dve.wait_ge(in_["rows"], 16)
                for t in tiles:
                    dve.wait_ge(set_pe, 5 + M + t)
                    tt(gates[:, t, :], bank_gates[t][:, 0:2 * C], gate_b, ALU.add).then_inc(set_dve, 1)

            def softmax(t, u):
                made(dve, scored[u], t)
                s = bank_s[u][:, :].rearrange("p (h k) -> p h k", h=HEADS)
                dve.tensor_reduce(u_max[u][:, :], s, AX_X, ALU.max).then_inc(max_ok[u], 1)
                made(dve, max_ok[u], t)
                made(dve, turned[u], t - 1)
                tt(u_p[u][:, :, :], s, u_max[u][:, :].unsqueeze(2).to_broadcast([P, HEADS, S]), ALU.subtract).then_inc(subtracted[u], 1)

            def normalise(t, u):
                made(dve, weighed[u], t)
                o = bank_o[u][:, 0:HEADS * VW].rearrange("p (h v) -> p h v", h=HEADS)
                dve.reciprocal(u_r[u][:, :], o[:, :, HD]).then_inc(r_ok[u], 1)
                made(dve, r_ok[u], t)
                made(dve, o_turned[u], t - 1)
                tt(u_o[u][:, :].rearrange("p (h d) -> p h d", h=HEADS), o[:, :, 0:HD],
                   u_r[u][:, :].unsqueeze(2).to_broadcast([P, HEADS, HD]), ALU.mult).then_inc(o_ok[u], 1)

            def z_read_qkv(t):
                made(dve, z_qkv, t)
                made(dve, scored[Z], t - 1)
                for s in range(2):
                    part = slice(s * P // 2, (s + 1) * P // 2)
                    tt(qs[part, Z, s, :].rearrange("p (b q) -> p b q", b=SEQS), bank_qkv0[part, 0:P].rearrange("p (b q) -> p b q", b=SEQS),
                       q_scale[part, bass.ts(t, SEQS)].unsqueeze(2).to_broadcast([P // 2, SEQS, S]), ALU.mult)
                made(dve, ks_ok[Z], t - 1)
                made(dve, z_kl_ok, t - 1)
                dve.tensor_copy(z_k[:, :], bank_qkv0[:, P:2 * P])
                made(dve, vs_ok[Z], t - 1)
                dve.tensor_copy(z_v[:, :, :, :].rearrange("p b g d -> p (b g d)"), bank_qkv0[:, 2 * P:3 * P]).then_inc(z_qkv_read, 1)

            def z_residual(t):
                made(dve, projected[Z], t)
                dve.wait_ge(x_b_ok, 1 if isinstance(t, int) and t == 0 else 2)
                tt(of_tile(x1, t), bank_o[Z][:, 0:C], of_tile(x_b, t), ALU.add).then_inc(y_read[Z], 1)

            def z_mean_square(t):
                made(dve, z_ss_ok, t)
                ts(z_ms[:, :], z_ss[:, :], 1.0 / C, RMS_EPS ** 2, ALU.mult, ALU.max).then_inc(z_ms_ok, 1)

            def z_norm(t):
                made(dve, z_rn_ok, t)
                made(dve, z_xn_turned, t - 1)
                ts(z_xn[:, :], of_tile(x1, t), z_rn[:, 0:1], None, ALU.mult).then_inc(z_xn_ok, 1)

            def z_modulate(t):
                made(dve, z_xn_turned, t)
                modulate(bank_x1[:, 0:P], SEQS, z_xs[:, :], z_hm[:, :], z_scaled, t + 1, z_hm_ok, 0, bass.ts(t, SEQS),
                         [(z_up1, t - 1), (z_up2, t - 1)])

            def z_hidden1(t):
                loaded(dve, "mlp", t)
                made(dve, z_up1, t)
                made(dve, z_g_ok, t - 1)
                tt(z_h1[:, :, :], bank_up1[:, :].rearrange("p (c t) -> p c t", c=FC),
                   w("mlp", "b1")[:, 0:FC].unsqueeze(2).to_broadcast([P, FC, P]), ALU.add).then_inc(z_h1_ok, 1)

            def z_silu(t):
                made(dve, z_th_ok, t)
                made(dve, z_h1_ok, t)
                stt(z_act[:, :, :], z_th[:, :, :], 1.0, z_h1[:, :, :], ALU.add, ALU.mult).then_inc(z_act_ok, 1)

            def z_gated(t):
                loaded(dve, "mlp", t)
                made(dve, z_act_ok, t)
                made(dve, z_up2, t)
                made(dve, z_down, t - 1)
                for c in range(FC):
                    last = stt(z_g[:, c, :], bank_up2[:, c * P:c * P + P], w("mlp", "b1")[:, FC + c:FC + c + 1], z_act[:, c, :],
                               ALU.add, ALU.mult)
                last.then_inc(z_g_ok, 1)

            def z_result(t):
                made(dve, z_down, t)
                made(dve, z_x1b_ok, t)
                stt(of_tile(x2, t), bank_down0[:, 0:C], 0.5, z_x1b[:, :], ALU.mult, ALU.add).then_inc(x2_ok, 1)

            def statistics(t, src, st, mv, ve, mv_ok, ve_ok):
                dve.drain()
                dve.bn_stats(st[:, :], src)
                dve.drain()
                dve.bn_aggr(mv[:, :], st[:, :]).then_inc(mv_ok, 1)
                made(dve, mv_ok, t)
                ts(ve[:, :], mv[:, 1:2], LN_EPS, None, ALU.add).then_inc(ve_ok, 1)

            def a_statistics(t):
                statistics(t, of_tile(x2, t), a_st, a_mv, a_ve, a_mv_ok, a_ve_ok)

            def a_norm(t):
                made(dve, a_rs_ok, t)
                made(dve, a_turned, t - 1)
                ts(a_xn[:, :], of_tile(x2, t), a_mv[:, 0:1], a_rs[:, 0:1], ALU.subtract, ALU.mult).then_inc(a_xn_ok, 1)

            def a_modulate(t):
                made(dve, a_turned, t)
                modulate(bank_x2[:, 0:P], SEQS, a_xs[:, :], a_h[:, :], a_scaled, t + 1, a_h_ok, 1, bass.ts(t, SEQS),
                         [(a_k_ps, t - 1), (a_q_ps, t - 1), (a_v_ps, t - 1)])

            def f_statistics(t):
                statistics(t, of_tile(x3, t), f_st, f_mv, f_ve, f_mv_ok, f_ve_ok)

            def f_norm(t):
                made(dve, f_rs_ok, t)
                made(dve, f_turned, t - 1)
                ts(f_xn[:, :], of_tile(x3, t), f_mv[:, 0:1], f_rs[:, 0:1], ALU.subtract, ALU.mult).then_inc(f_xn_ok, 1)

            def f_modulate(t):
                made(dve, f_turned, t)
                modulate(bank_x3[:, 0:P], SEQS, f_xs[:, :], f_h[:, :], f_scaled, t + 1, f_h_ok, 2, bass.ts(t, SEQS),
                         [(f_up1, t - 1), (f_up3, t - 1)])

            def a_logits(t):
                for m in range(M):
                    made(dve, y_read[m], t)
                logits = a_y[:, :, C:C + M].rearrange("p m j -> p j m")
                dve.tensor_reduce(a_lg[:, :], logits, AX_X, ALU.add).then_inc(a_lg_ok, 1)
                made(dve, a_lg_ok, t)
                tt(a_lb[:, :], a_lg[:, :], fus_bg, ALU.add).then_inc(a_lb_ok, 1)
                made(dve, a_lb_ok, t)
                dve.tensor_reduce(a_lm[:, :], a_lb[:, :], AX_X, ALU.max, negate=True).then_inc(a_lm_ok, 1)

            def a_gate(t):
                made(dve, a_le_ok, t)
                dve.reciprocal(a_lr[:, :], a_ls[:, :]).then_inc(a_lr_ok, 1)
                ts(a_f[:, 0, :], a_y[:, 0, 0:C], a_le[:, 0:1], None, ALU.mult).then_inc(a_f_ok, 1)
                for m in range(1, M):
                    dve.wait_ge(a_f_ok, M * t + m)
                    stt(a_f[:, m, :], a_y[:, m, 0:C], a_le[:, m:m + 1], a_f[:, m - 1, :], ALU.mult, ALU.add).then_inc(a_f_ok, 1)
                made(dve, a_lr_ok, t)
                dve.wait_ge(a_f_ok, M * t + M)
                stt(a_fg[:, :], a_f[:, M - 1, :], a_lr[:, 0:1], of_tile(gates, t)[:, 0:C], ALU.mult, ALU.mult).then_inc(a_fg_ok, 1)
                made(dve, a_fg_ok, t)
                tt(of_tile(x3, t), a_fg[:, :], of_tile(x2, t), ALU.add).then_inc(x3_ok, 1)

            def f_silu(t):
                made(dve, f_th_ok, t)
                made(dve, f_g_ok, t - 1)
                stt(f_v[:, :], f_th[:, :], 1.0, bank_w1[:, :], ALU.add, ALU.mult).then_inc(f_v_ok, 1)

            def f_gated(t):
                made(dve, f_v_ok, t)
                made(dve, f_up3, t)
                made(dve, f_down, t - 1)
                tt(f_g[:, :, :].rearrange("p c t -> p (c t)"), f_v[:, :], bank_w3[:, :], ALU.mult).then_inc(f_g_ok, 1)

            def f_result(t):
                made(dve, f_down, t)
                stt(f_y[:, :], bank_down1[:, 0:C], 0.5, of_tile(gates, t)[:, C:2 * C], ALU.mult, ALU.mult).then_inc(f_y_ok, 1)
                made(dve, f_y_ok, t)
                tt(of_tile(x4, t), f_y[:, :], of_tile(x3, t), ALU.add).then_inc(x4_ok, 1)

            def run(i, stage, step, *of):
                if exists(i - stage):
                    step(i - stage, *of)

            def iteration(i):
                run(i, 0, z_read_qkv)
                if at(i, 0):
                    setup_ada()
                    first_mean_square(1, 1, TILES)
                run(i, 2, normalise, 1)
                run(i, 1, z_result)
                if at(i, 1):
                    setup_gates((7,))
                run(i, 1, a_statistics)
                run(i, 2, normalise, 0)
                run(i, 2, normalise, 2)
                run(i, 2, normalise, 3)
                run(i, 1, a_norm)
                run(i, 0, softmax, Z)
                if at(i, 0):
                    first_norm(1, 1, TILES)
                    setup_gates((0, 1))
                run(i, 1, a_modulate)
                run(i, 2, a_logits)
                run(i, 2, a_gate)
                run(i, 0, normalise, Z)
                if at(i, 0):
                    first_modulate(1)
                run(i, 2, f_statistics)
                run(i, 2, f_norm)
                run(i, 0, z_residual)
                if at(i, 0):
                    setup_gates((2,))
                run(i, 0, z_mean_square)
                run(i, 2, f_modulate)
                run(i, 0, z_norm)
                if at(i, 0):
                    setup_gates((3, 4,))
                run(i, 1, softmax, 0)
                run(i, 0, z_modulate)
                if at(i, 0):
                    first_modulate(2)
                run(i, 1, softmax, 1)
                run(i, 1, softmax, 2)
                run(i, 0, z_hidden1)
                run(i, 2, f_silu)
                run(i, 2, f_gated)
                run(i, 1, softmax, 3)
                run(i, 0, z_silu)
                run(i, 0, z_gated)
                if at(i, 0):
                    setup_gates((5,6,))
                run(i, 2, f_result)

            for i in range(STAGES):
                iteration(i)
            with dve.Fori(STAGES, TILES) as i:
                iteration(i)
            for i in range(TILES, TILES + STAGES - 1):
                iteration(i)

        @block.scalar
        def _(act):
            act.wait_ge(in_["cond"], 16)
            act.activation(cond_tanh[:, :], cond_sb[:, :], ACT.Tanh, scale=0.5).then_inc(set_act, 1)
            act.wait_ge(in_x, 16)
            act.activation(n_sq[:, 0, :], x_in[:, 0, :], ACT.Square, accum_out=n_ss[:, 0:1]).then_inc(n_ss_ok, 1)
            act.wait_ge(set_pe, 2)
            act.activation(cond_t[:, :], bank_c1[:, 0:B], ACT.Copy, scale=0.5).then_inc(set_act, 1)

            def setup_squares():
                act.wait_ge(set_act, 2)
                act.copy(cond_tok[:, :, :], cond_t[:, :].unsqueeze(2).to_broadcast([P, B, S])).then_inc(set_act, 1)
                act.wait_ge(in_x_rest, 16)
                for t in range(1, TILES):
                    last = act.activation(n_sq[:, t, :], x_in[:, t, :], ACT.Square, accum_out=n_ss[:, t:t + 1])
                last.then_inc(n_ss_ok, 1)

            def setup_fused():
                for m in range(M):
                    act.wait_ge(set_pe, 5 + m)
                    act.copy(wo_fused[:, m, :], banks_wo[m][:, 0:C + M]).then_inc(set_act, 1)

            def exponential(t, u):
                made(act, subtracted[u], t)
                p = u_p[u][:, :, :].rearrange("p h k -> p (h k)")
                act.activation(p, p, ACT.Exp).then_inc(exp_ok[u], 1)

            def take_turned(t, u):
                made(act, turned[u], t)
                made(act, weighed[u], t - 1)
                act.copy(u_pt[u][:, :, :].rearrange("p g t -> p (g t)"), bank_t[u][:, :]).then_inc(pt_ok[u], 1)

            def take_out(t, u):
                made(act, o_turned[u], t)
                made(act, projected[u], t - 1)
                act.copy(u_ot[u][:, :], bank_o[u][:, 0:P]).then_inc(ot_ok[u], 1)

            def take_y(t, m):
                made(act, projected[m], t)
                made(act, a_fg_ok, t - 1)
                act.copy(a_y[:, m, :], bank_o[m][:, 0:C + M]).then_inc(y_read[m], 1)

            def z_take_h(t):
                act.wait_ge(n_h_ok, 1 + sum(begin <= t for begin, _ in PARTS[1:]) if isinstance(t, int) else len(PARTS))
                made(act, z_qkv, t - 1)
                act.copy(z_h[:, :], of_tile(n_h, t)).then_inc(z_h_ok, 1)

            def z_spread_lower(t):
                made(act, z_qkv_read, t)
                made(act, scored[Z], t - 1)
                for s in range(SLOTS // 2):
                    last = act.activation(ks[:, Z, s, :], z_k[:, :], ACT.Copy, scale=slot_mask[:, s:s + 1])
                last.then_inc(z_kl_ok, 1)

            def z_square(t):
                made(act, y_read[Z], t)
                made(act, z_ms_ok, t - 1)
                act.activation(z_sq[:, :], of_tile(x1, t), ACT.Square, accum_out=z_ss[:, :]).then_inc(z_ss_ok, 1)

            def z_tanh(t):
                made(act, z_h1_ok, t)
                made(act, z_act_ok, t - 1)
                act.activation(z_th[:, :, :], z_h1[:, :, :], ACT.Tanh, scale=0.5).then_inc(z_th_ok, 1)

            def a_take_q(t):
                made(act, a_q_ps, t)
                for m in range(M):
                    made(act, scored[m], t - 1)
                q_ps = bank_q[:, :].rearrange("p (m t) -> p m t", m=M)
                half = P // 2
                act.activation(qs[0:half, 0:M, 0, :], q_ps[0:half], ACT.Copy, scale=SCALE)
                act.activation(qs[half:P, 0:M, 1, :], q_ps[half:P], ACT.Copy, scale=SCALE).then_inc(a_q_ok, 1)

            def a_take_k(t):
                made(act, a_k_ps, t)
                for m in range(M):
                    made(act, ks_ok[m], t - 1)
                act.copy(a_k[:, :, :].rearrange("p m t -> p (m t)"), bank_k[:, :]).then_inc(a_k_ok, 1)

            def a_spread_lower(t, part):
                if part == 0:
                    made(act, a_k_ps, t)
                    for m in range(M):
                        made(act, scored[m], t - 1)
                for s in (2 * part, 2 * part + 1):
                    last = act.activation(ks[:, 0:M, s, :], bank_k[:, :].rearrange("p (m t) -> p m t", m=M), ACT.Copy,
                                          scale=slot_mask[:, s:s + 1])
                if part == 1:
                    last.then_inc(a_kl_ok, 1)

            def a_take_v(t):
                made(act, a_v_ps, t)
                for m in range(M):
                    made(act, vs_ok[m], t - 1)
                act.copy(a_v[:, :, :, :, :].rearrange("p m b g d -> p (m b g d)"), bank_v[:, :]).then_inc(a_v_ok, 1)

            def a_gate_exp(t):
                made(act, a_lm_ok, t)
                act.activation(a_le[:, :], a_lb[:, :], ACT.Exp, bias=a_lm[:, 0:1], accum_out=a_ls[:, :]).then_inc(a_le_ok, 1)

            def f_tanh(t):
                made(act, f_up1, t)
                made(act, f_v_ok, t - 1)
                act.activation(f_th[:, :], bank_w1[:, :], ACT.Tanh, scale=0.5).then_inc(f_th_ok, 1)

            def run(i, stage, step, *of):
                if exists(i - stage):
                    step(i - stage, *of)

            def iteration(i):
                run(i, 0, z_take_h)
                if at(i, 0):
                    setup_squares()
                run(i, 2, take_turned, 0)
                run(i, 2, take_turned, 1)
                run(i, 2, exponential, 3)
                run(i, 2, take_turned, 2)
                run(i, 2, take_turned, 3)
                run(i, 0, z_spread_lower)
                if at(i, 0):
                    setup_fused()
                run(i, 2, take_out, 1)
                run(i, 2, take_out, 0)
                run(i, 2, take_out, 2)
                run(i, 2, take_out, 3)
                run(i, 2, take_y, 1)
                run(i, 2, take_y, 0)
                run(i, 2, take_y, 2)
                run(i, 2, take_y, 3)
                run(i, 0, exponential, Z)
                run(i, 2, a_gate_exp)
                run(i, 1, a_take_k)
                run(i, 0, take_turned, Z)
                run(i, 1, a_spread_lower, 0)
                run(i, 1, a_spread_lower, 1)
                run(i, 0, take_out, Z)
                run(i, 1, a_take_q)
                run(i, 0, z_square)
                run(i, 1, exponential, 0)
                run(i, 1, a_take_v)
                run(i, 1, exponential, 1)
                run(i, 2, f_tanh)
                run(i, 1, exponential, 2)
                run(i, 0, z_tanh)

            for i in range(STAGES):
                iteration(i)
            with act.Fori(STAGES, TILES) as i:
                iteration(i)
            for i in range(TILES, TILES + STAGES - 1):
                iteration(i)

        @block.gpsimd
        def _(pool):
            tt = pool.tensor_tensor

            pool.memset(qs[:, :, :, :], 0.0).then_inc(set_pool, 1)
            pool.wait_ge(set_dve, 2)

            def first_power(part, begin, end):
                pool.wait_ge(n_ms_ok, part + 1)
                tt(out=n_rn[:, begin:end], in0=n_ms[:, begin:end], in1=neg_half[:, begin:end], op=ALU.pow).then_inc(n_rn_ok, 1)

            def add_bias(begin, end):
                proj_b = packs["rows"][0][:, packs["rows"][1]["proj_b"]]
                tt(out=x_b[:, begin:end, :], in0=x_in[:, begin:end, :], in1=proj_b.unsqueeze(1).to_broadcast([P, end - begin, C]),
                   op=ALU.add).then_inc(x_b_ok, 1)

            first_power(0, 0, 1)

            def setup_power():
                first_power(1, 1, TILES)

            def setup_bias():
                pool.wait_ge(in_["rows"], 16)
                pool.wait_ge(in_x_rest, 16)
                add_bias(0, 1)
                add_bias(1, TILES)

            def power(t, src, out_, ready, done):
                made(pool, ready, t)
                tt(out=out_[:, :], in0=src[:, :], in1=neg_half[:, 0:1], op=ALU.pow).then_inc(done, 1)

            def spread_upper(t, u):
                made(pool, z_qkv_read if u == Z else a_k_ok, t)
                made(pool, scored[u], t - 1)
                k = (z_k[:, :] if u == Z else a_k[:, u, :]).unsqueeze(1).to_broadcast([P, SLOTS // 2, P])
                upper = slice(SLOTS // 2, SLOTS)
                tt(out=ks[:, u, upper, :], in0=k, in1=slot_mask[:, upper].unsqueeze(2).to_broadcast([P, SLOTS // 2, P]), op=ALU.mult)\
                    .then_inc(ks_ok[u], 1)

            def spread_values(t, u):
                if u == Z:
                    made(pool, z_qkv_read, t)
                else:
                    made(pool, a_v_ok, t)
                made(pool, weighed[u], t - 1)
                view = [P, SEQS * G, J, HD]
                v = z_v[:, :, :, :] if u == Z else a_v[:, u, :, :, :]
                tt(out=vs[:, u, :, :, :, 0:HD].rearrange("p b g j d -> p (b g) j d"),
                   in0=v.rearrange("p b g d -> p (b g) d").unsqueeze(2).to_broadcast(view),
                   in1=j_mask.unsqueeze(1).unsqueeze(3).to_broadcast(view), op=ALU.mult).then_inc(vs_ok[u], 1)

            def z_power(t):
                power(t, z_ms, z_rn, z_ms_ok, z_rn_ok)

            def a_power(t):
                power(t, a_ve, a_rs, a_ve_ok, a_rs_ok)

            def f_power(t):
                power(t, f_ve, f_rs, f_ve_ok, f_rs_ok)

            def z_add_mlp_bias(t):
                made(pool, y_read[Z], t)
                made(pool, x2_ok, t - 1)
                tt(out=z_x1b[:, :], in0=of_tile(x1, t), in1=packs["rows"][0][:, packs["rows"][1]["mlp_b2"]], op=ALU.add)\
                    .then_inc(z_x1b_ok, 1)

            def run(i, stage, step, *of):
                if exists(i - stage):
                    step(i - stage, *of)

            def iteration(i):
                run(i, 1, z_add_mlp_bias)
                run(i, 2, spread_values, 0)
                run(i, 2, spread_values, 2)
                run(i, 0, spread_upper, Z)
                run(i, 1, a_power)
                run(i, 0, spread_values, Z)
                if at(i, 0):
                    setup_power()
                    setup_bias()
                run(i, 1, spread_upper, 3)
                run(i, 1, spread_upper, 0)
                run(i, 2, f_power)
                run(i, 1, spread_upper, 1)
                run(i, 0, z_power)
                run(i, 1, spread_upper, 2)
                run(i, 1, spread_values, 1)
                run(i, 1, spread_values, 3)

            for i in range(STAGES):
                iteration(i)
            with pool.Fori(STAGES, TILES) as i:
                iteration(i)
            for i in range(TILES, TILES + STAGES - 1):
                iteration(i)


def kernel(**inputs):
    import numpy as np
    import concourse.bacc as bacc
    from concourse.bass_utils import run_bass_kernel_spmd

    a = {k: np.asarray(v) for k, v in inputs.items()}

    def col(v):
        return v.reshape(-1, P).T

    def chunks(m):
        return m.reshape(-1, P, m.shape[1]).transpose(1, 0, 2).reshape(P, -1)

    p = np.arange(P)
    q, k = np.arange(S)[:, None], np.arange(S)[None, :]
    dist = np.abs(q - k)
    bias = [-dist, np.where(dist <= 1, 0.0, -1e9), np.where(q // 2 == k // 2, 0.0, -1e9)]

    def parts(v):
        rest, out = v.astype(np.float32), []
        for _ in range(3):
            part = (rest.view(np.uint32) & np.uint32(0xFFFF0000)).view(np.float32)
            out.append(part)
            rest = rest - part
        return np.concatenate([*out, np.zeros_like(rest)])

    const = {
        "ident": np.eye(P), "same_q": p[:, None] % S == p[None, :] % S, "same_b": p[:, None] // S == p[None, :] // S,
        "key_of": p[:, None] % S == k, "bias": np.concatenate([parts(b) for b in bias], 1),
        "slot_mask": (p[:, None] // HD) % SLOTS == np.arange(SLOTS), "j_mask": p[:, None] // S == np.arange(J),
    }

    def pack(*cols):
        return np.ascontiguousarray(np.concatenate(cols, 1))

    heads = ("grid", "reg", "ent", "sem")
    arrays = {
        "x": a["x"].reshape(-1, C),
        "cond": a["cond_1024"],
        "mask": np.ascontiguousarray(a["mask_BxS_ik0"].reshape(-1, P).T),
        "early": pack(*[const[n].astype(np.float32) for n in ("ident", "same_q", "same_b", "key_of", "bias", "slot_mask", "j_mask")],
                      a["L0_cond_shift_w"].T, a["L0_cond_scale_w"].T,
                      col(a["L0_cond_norm_w"]), col(a["L0_cond_scale_b"]), col(a["L0_cond_shift_b"])),
        "l0": pack(a["L0_cond_qkv_w"].T, a["L0_cond_proj_w"].T),
        "mlp": pack(a["L0_cond_mlp_w1"].T, chunks(a["L0_cond_mlp_w2"].T), col(a["L0_cond_mlp_b1"])),
        "ada": pack(a["L1_cond_ada_w"], col(a["L1_cond_ada_b"]), *[col(a[f"L1_cond_{n}"]) for n in ("ln1_g", "ln1_b", "ln2_g", "ln2_b")],
                    a["L1_cond_fus_wo"], chunks(a["L1_cond_fus_wg"]), *[a[f"L1_cond_{h}_wo"].T for h in heads]),
        "qkv1": pack(*[a[f"L1_cond_{h}_{n}"] for n in ("wq", "wk", "wv") for h in heads]),
        "ffn": pack(a["L1_cond_ffn_w1"], a["L1_cond_ffn_w3"], chunks(a["L1_cond_ffn_w2"])),
        "rows": np.ascontiguousarray(np.concatenate([a["L0_cond_proj_b"], a["L0_cond_mlp_b2"], a["L1_cond_ada_b"][2 * C:3 * C],
                                                     a["L1_cond_ada_b"][5 * C:6 * C], a["L1_cond_fus_bg"]])[None, :]),
    }
    nc = bacc.Bacc("TRN2", target_bir_lowering=False, num_devices=1)
    args = [nc.dram_tensor(f"in_{n}", v.shape, mybir.dt.from_np(v.dtype), kind="ExternalInput").ap() for n, v in arrays.items()]
    out = nc.dram_tensor("out_x", arrays["x"].shape, F32, kind="ExternalOutput").ap()
    build(nc, *args, out)
    r = run_bass_kernel_spmd(nc, [{f"in_{n}": v for n, v in arrays.items()}], core_ids=[0])
    return r.results[0]["out_x"].reshape(a["x"].shape)
```
